# Optimizing a Trainium2 kernel written in Bass

```python
import numpy as np
import jax
import jax.numpy as jnp

def _softmax(x, axis=-1):
    return jax.nn.softmax(x, axis=axis)

def _gelu(x):
    return jax.nn.gelu(x, approximate=True)

def _silu(x):
    return jax.nn.silu(x)

def _sigmoid(x):
    return jax.nn.sigmoid(x)

def _layernorm(x, axis=-1, eps=1e-05):
    m = jnp.mean(x, axis=axis, keepdims=True)
    v = jnp.var(x, axis=axis, keepdims=True)
    return (x - m) / jnp.sqrt(v + eps)

def _scatter_add(tgt, idx, src, axis=0):
    return tgt.at[idx].add(src)

def _segment_sum(src, seg, n):
    return jax.ops.segment_sum(src, seg, n)
kernel_name = 'mk_vit_tower_d1_tok_img768_r4_c83518'

def setup_inputs(seed: int=0):
    np.random.seed(seed)
    _w = jnp.asarray

    def _rec_inputs():
        import jax
        import jax.numpy as jnp
        _rk = jax.random.key(seed)
        x = 7.57192e-06 + 1.00007 * jax.random.normal(jax.random.fold_in(_rk, 1), (64, 3, 224, 224), jnp.float32)
        return x
    x = _rec_inputs()

    def _L0_tok_setup():
        import jax, jax.numpy as jnp
        import numpy as np
        P = 16

        def _patchify(x, p):
            B, C, H, W = x.shape
            Hb, Wb = (H // p, W // p)
            x = x.reshape(B, C, Hb, p, Wb, p)
            x = jnp.transpose(x, (0, 2, 4, 1, 3, 5))
            return x.reshape(B, Hb * Wb, C * p * p)
        key = jax.random.key(seed)
        k1, k2 = jax.random.split(key)
        B, C, H, W = (64, 3, 224, 224)
        patch_dim, embed_dim = (C * P * P, 192)
        x = jax.random.normal(k1, (B, C, H, W), dtype=jnp.float32)
        Wt = jax.random.normal(k2, (embed_dim, patch_dim), dtype=jnp.float32) * (1.0 / np.sqrt(patch_dim))
        b = jnp.zeros((embed_dim,), dtype=jnp.float32)
        return {'x': x, 'W': Wt, 'b': b}
    _L0_tok_all = _L0_tok_setup()
    _L0_tok_in = {k: v for k, v in _L0_tok_all.items() if k in ('W', 'b')}
    del _L0_tok_all

    def _L0_attn_setup():
        import jax, jax.numpy as jnp
        import numpy as np
        EMBED_DIM = 192
        NUM_HEADS = 12
        HEAD_DIM = EMBED_DIM // NUM_HEADS
        MAX_WAVELENGTH = 10000.0
        ROPE_PERCENT = 0.5

        def p_rope(x, positions):
            rope_angles = int(ROPE_PERCENT * HEAD_DIM) // 2
            nope_angles = HEAD_DIM // 2 - rope_angles
            fraction = 2.0 * jnp.arange(rope_angles, dtype=x.dtype) / HEAD_DIM
            timescale = MAX_WAVELENGTH ** fraction
            timescale = jnp.concatenate([timescale, jnp.full((nope_angles,), jnp.inf, dtype=x.dtype)])
            sinusoid = positions[:, None] / timescale[None, :]
            sin, cos = (jnp.sin(sinusoid), jnp.cos(sinusoid))
            x1, x2 = jnp.split(x, 2, axis=-1)
            return jnp.concatenate([x1 * cos - x2 * sin, x2 * cos + x1 * sin], axis=-1)

        def _shape(x, B, S):
            return x.reshape(B, S, NUM_HEADS, HEAD_DIM).transpose(0, 2, 1, 3).reshape(B * NUM_HEADS, S, HEAD_DIM)
        key = jax.random.key(seed)
        ks = jax.random.split(key, 9)
        B, T, E = (16, 256, EMBED_DIM)
        s = 0.02
        return {'hidden_states': jax.random.normal(ks[0], (B, T, E), jnp.float32), 'wq': jax.random.normal(ks[1], (E, E), jnp.float32) * s, 'bq': jax.random.normal(ks[2], (E,), jnp.float32) * s, 'wk': jax.random.normal(ks[3], (E, E), jnp.float32) * s, 'bk': jax.random.normal(ks[4], (E,), jnp.float32) * s, 'wv': jax.random.normal(ks[5], (E, E), jnp.float32) * s, 'bv': jax.random.normal(ks[6], (E,), jnp.float32) * s, 'wo': jax.random.normal(ks[7], (E, E), jnp.float32) * s, 'bo': jax.random.normal(ks[8], (E,), jnp.float32) * s}
    _L0_attn_all = _L0_attn_setup()
    _L0_attn_in = {k: v for k, v in _L0_attn_all.items() if k in ('wq', 'bq', 'wk', 'bk', 'wv', 'bv', 'wo', 'bo')}
    del _L0_attn_all

    def _L0_ffn_setup():
        import jax, jax.numpy as jnp
        import numpy as np
        B, T, E = (2, 256, 192)
        H = 768
        N_EXP = 4
        key = jax.random.key(seed)
        ks = jax.random.split(key, 8)
        s_e = 1.0 / np.sqrt(E)
        s_h = 1.0 / np.sqrt(H)
        return {'x': jax.random.normal(ks[0], (B, T, E), dtype=jnp.float32), 'Wg': jax.random.uniform(ks[1], (E, N_EXP), minval=-s_e, maxval=s_e, dtype=jnp.float32), 'bg': jax.random.uniform(ks[2], (N_EXP,), minval=-s_e, maxval=s_e, dtype=jnp.float32), 'W1': jax.random.uniform(ks[3], (N_EXP, E, H), minval=-s_e, maxval=s_e, dtype=jnp.float32), 'b1': jax.random.uniform(ks[4], (N_EXP, H), minval=-s_e, maxval=s_e, dtype=jnp.float32), 'W2': jax.random.uniform(ks[5], (N_EXP, H, E), minval=-s_h, maxval=s_h, dtype=jnp.float32), 'b2': jax.random.uniform(ks[6], (N_EXP, E), minval=-s_h, maxval=s_h, dtype=jnp.float32)}
    _L0_ffn_all = _L0_ffn_setup()
    _L0_ffn_in = {k: v for k, v in _L0_ffn_all.items() if k in ('Wg', 'bg', 'W1', 'b1', 'W2', 'b2')}
    del _L0_ffn_all
    return {'x': x, 'L0_tok_W': _L0_tok_in['W'], 'L0_tok_b': _L0_tok_in['b'], 'L0_attn_wq': _L0_attn_in['wq'], 'L0_attn_bq': _L0_attn_in['bq'], 'L0_attn_wk': _L0_attn_in['wk'], 'L0_attn_bk': _L0_attn_in['bk'], 'L0_attn_wv': _L0_attn_in['wv'], 'L0_attn_bv': _L0_attn_in['bv'], 'L0_attn_wo': _L0_attn_in['wo'], 'L0_attn_bo': _L0_attn_in['bo'], 'L0_ffn_Wg': _L0_ffn_in['Wg'], 'L0_ffn_bg': _L0_ffn_in['bg'], 'L0_ffn_W1': _L0_ffn_in['W1'], 'L0_ffn_b1': _L0_ffn_in['b1'], 'L0_ffn_W2': _L0_ffn_in['W2'], 'L0_ffn_b2': _L0_ffn_in['b2']}

def reference(x, L0_tok_W, L0_tok_b, L0_attn_wq, L0_attn_bq, L0_attn_wk, L0_attn_bk, L0_attn_wv, L0_attn_bv, L0_attn_wo, L0_attn_bo, L0_ffn_Wg, L0_ffn_bg, L0_ffn_W1, L0_ffn_b1, L0_ffn_W2, L0_ffn_b2):
    import jax
    import jax.numpy as jnp

    def _L0_tok_ref(x, W, b):
        import jax, jax.numpy as jnp
        import numpy as np
        P = 16

        def _patchify(x, p):
            B, C, H, W = x.shape
            Hb, Wb = (H // p, W // p)
            x = x.reshape(B, C, Hb, p, Wb, p)
            x = jnp.transpose(x, (0, 2, 4, 1, 3, 5))
            return x.reshape(B, Hb * Wb, C * p * p)
        patches = _patchify(x, P)
        return jnp.einsum('bnd,ed->bne', patches, W) + b

    def _L0_attn_ref(hidden_states, wq, bq, wk, bk, wv, bv, wo, bo):
        import jax, jax.numpy as jnp
        import numpy as np
        EMBED_DIM = 192
        NUM_HEADS = 12
        HEAD_DIM = EMBED_DIM // NUM_HEADS
        MAX_WAVELENGTH = 10000.0
        ROPE_PERCENT = 0.5

        def p_rope(x, positions):
            rope_angles = int(ROPE_PERCENT * HEAD_DIM) // 2
            nope_angles = HEAD_DIM // 2 - rope_angles
            fraction = 2.0 * jnp.arange(rope_angles, dtype=x.dtype) / HEAD_DIM
            timescale = MAX_WAVELENGTH ** fraction
            timescale = jnp.concatenate([timescale, jnp.full((nope_angles,), jnp.inf, dtype=x.dtype)])
            sinusoid = positions[:, None] / timescale[None, :]
            sin, cos = (jnp.sin(sinusoid), jnp.cos(sinusoid))
            x1, x2 = jnp.split(x, 2, axis=-1)
            return jnp.concatenate([x1 * cos - x2 * sin, x2 * cos + x1 * sin], axis=-1)

        def _shape(x, B, S):
            return x.reshape(B, S, NUM_HEADS, HEAD_DIM).transpose(0, 2, 1, 3).reshape(B * NUM_HEADS, S, HEAD_DIM)
        B, T, E = hidden_states.shape
        scaling = HEAD_DIM ** (-0.5)
        q = (hidden_states @ wq.T + bq) * scaling
        k = hidden_states @ wk.T + bk
        v = hidden_states @ wv.T + bv
        q = _shape(q, B, T)
        k = _shape(k, B, T)
        v = _shape(v, B, T)
        positions = jnp.arange(T, dtype=hidden_states.dtype)
        k = p_rope(k, positions)
        q = p_rope(q, positions)
        attn = jnp.einsum('bqd,bkd->bqk', q, k)
        attn = jax.nn.softmax(attn, axis=-1)
        out = jnp.einsum('bqk,bkd->bqd', attn, v)
        out = out.reshape(B, NUM_HEADS, T, HEAD_DIM).transpose(0, 2, 1, 3).reshape(B, T, E)
        return out @ wo.T + bo

    def _L0_ffn_ref(x, Wg, bg, W1, b1, W2, b2):
        import jax, jax.numpy as jnp
        import numpy as np
        B, T, E = (2, 256, 192)
        H = 768
        N_EXP = 4
        gate_logits = jnp.einsum('bte,en->btn', x, Wg) + bg
        top = jnp.argmax(gate_logits, axis=-1)
        h = jax.nn.gelu(jnp.einsum('bte,neh->nbth', x, W1) + b1[:, None, None, :], approximate=False)
        y = jnp.einsum('nbth,nhe->nbte', h, W2) + b2[:, None, None, :]
        onehot = jax.nn.one_hot(top, N_EXP, dtype=x.dtype)
        out = jnp.einsum('nbte,btn->bte', y, onehot)
        return out
    h = _L0_tok_ref(x, L0_tok_W, L0_tok_b)
    h = h + _L0_attn_ref(_layernorm(h, axis=-1), L0_attn_wq, L0_attn_bq, L0_attn_wk, L0_attn_bk, L0_attn_wv, L0_attn_bv, L0_attn_wo, L0_attn_bo)
    h = h + _L0_ffn_ref(_layernorm(h, axis=-1), L0_ffn_Wg, L0_ffn_bg, L0_ffn_W1, L0_ffn_b1, L0_ffn_W2, L0_ffn_b2)
    return h

_drawn_inputs = setup_inputs


def setup_inputs(seed=0):
    import zlib

    import numpy as np

    out = dict(_drawn_inputs(seed))
    spreads = {'L0_tok_b': (0.0, 0.1)}
    factors = {'L0_attn_wq': 8.0,
     'L0_attn_bq': 8.0,
     'L0_attn_wk': 8.0,
     'L0_attn_bk': 8.0,
     'L0_attn_wv': 2.728,
     'L0_attn_bv': 5.666,
     'L0_attn_wo': 2.744,
     'L0_ffn_b1': 3.914,
     'L0_ffn_b2': 2.688}
    for name, (base, spread) in spreads.items():
        noise = np.random.default_rng([zlib.crc32(name.encode()), seed]).standard_normal(out[name].shape)
        drawn = base * np.exp(spread * noise) if base else spread * noise
        out[name] = jnp.asarray(drawn.astype(out[name].dtype))
    for name, factor in factors.items():
        out[name] = (out[name] * factor).astype(out[name].dtype)
    return out
```

```python
from contextlib import ExitStack

import concourse.bass as bass
import numpy as np
from concourse import mybir
from concourse.alu_op_type import AluOpType as ALU

F32 = mybir.dt.float32
BF16 = mybir.dt.bfloat16
I32 = mybir.dt.int32
U32 = mybir.dt.uint32
ACT = mybir.ActivationFunctionType
AX = mybir.AxisListType

B, CH, IMG, PATCH = 64, 3, 224, 16
E, NH, HD = 192, 12, 16
NE, HID = 4, 768
SIDE = IMG // PATCH
TOK = SIDE * SIDE
NTOK = B * TOK
PD = CH * PATCH * PATCH
GI = 4
NG = B // GI
GT = GI * TOK
TP = 112
NT = GT // TP
QC = TOK // 2
KC = E // 2
PJ = PD // 128
HG = KC // HD
HALF = GT // 2
CAP = 98 * 128
FT = 128
NFT = 102
LIST = NE * CAP + 4 * FT
FILLS = 12
ROW = E + 2
EPS = 1e-5
Q_PARTS = [0, 0, 1, 0, 2, 1]
K_PARTS = [0, 1, 0, 2, 0, 1]
NSPLIT = len(Q_PARTS)
SK = NSPLIT * HD
assert NTOK <= CAP and NTOK // FT + NE - 1 <= NFT and LIST % (128 * FILLS) == 0 and SK + 2 <= 128

S_IN_SLOT = [2, 1, 2, 1, 2, 1, 2, 1, 0, 0, 0, 0]
S_HEADS = [list(range(sum(S_IN_SLOT[:s]), sum(S_IN_SLOT[:s + 1]))) for s in range(NH)]
A_TILES = [(0, 1), (2, 3), (4, 5), (6,)]
WO_TILES = [(5, 6), (0,), (1, 2), (3, 4)]
D_TILES = [(3, 4), (5, 6), (0,), (1, 2)]


def jobs_of(step, make_next, finish_prev, attend, attend_next):
    out = []
    if make_next:
        tiles = A_TILES[step]
        for n, t in enumerate(tiles):
            out += [(n, "patch", t), (n + 1, "norm", t), (n + 2, "trH", t), (n + 4, "qk", t),
                    (n + 7, "trQ", t)]
        if step == 3:
            out += [(5, "V", 0), (6, "V", 1), (8, "V", 2), (9, "V", 3)]
    if finish_prev[0]:
        out += [(3, "trO", 0), (4, "trO", 1), (6, "trN", 0)]
    if finish_prev[1]:
        out += [(10, "wo", WO_TILES[step])]
    if finish_prev[2]:
        out += [(5 + n, "D", t) for n, t in enumerate(D_TILES[step])]
        if step == 1:
            out += [(7, "route", 0)]
    if attend_next:
        out += [(8, "negmax", 0), (9, "trM", 0)]
    order = sorted(range(len(out)), key=lambda k: (out[k][0], k))
    return [out[k] for k in order]


PROLOGUE = [(0, job, t) for t in range(NT) for job in ("patch", "norm", "trH", "qk", "trQ")]
PROLOGUE += [(0, "V", m) for m in range(GI)]


def body_jobs(kind):
    if kind == "prologue":
        return [PROLOGUE, [(0, "negmax", 0), (1, "trM", 0)]]
    if kind == "tail":
        return [jobs_of(0, False, (True, True, True), False, False),
                jobs_of(1, False, (False, False, True), False, False)]
    out = []
    for i in range(GI):
        first, last = kind == "first", kind == "last"
        done = (not (first and i == 0), not (first and i == 0), not (first and i <= 1))
        out.append(jobs_of(i, not last, done, True, not (last and i == 3)))
    return out


WORK_JOBS = ("patch", "trH", "qk", "trQ", "V", "trO", "trN", "wo", "trM", "route")
WORK_BANKS = 3
KINDS = ["prologue", "first", "mid", "last", "tail"]


def work_table(kind):
    count, table = [0] * WORK_BANKS, {}
    n = 0
    for i, jobs in enumerate(body_jobs(kind)):
        for _, job, arg in jobs:
            if job in WORK_JOBS:
                b = n % WORK_BANKS
                table[(i, job, arg)] = (b, count[b])
                count[b] += 1
                n += 1
    return table, count


TABLES = {k: work_table(k) for k in KINDS}


def uses_before(kind, g, b):
    c = {k: TABLES[k][1][b] for k in KINDS}
    if kind == "prologue":
        return 0
    if kind == "first":
        return c["prologue"]
    if kind == "mid":
        return (g - 1) * c["mid"] + (c["prologue"] + c["first"])
    n = c["prologue"] + c["first"] + (NG - 2) * c["mid"]
    return n if kind == "last" else n + c["last"]


def wait(eng, sem, value):
    if not (isinstance(value, int) and value <= 0):
        eng.wait_ge(sem, value)


class Body:

    def __init__(self, kind, g, parity, earlier=None, earlier_prev=None):
        self.kind, self.g, self.parity = kind, g, parity
        self.earlier = g // 2 if earlier is None else earlier
        self.earlier_prev = (g - 1) // 2 if earlier is None else earlier_prev
        self.next = g + 1 if kind != "prologue" else 0
        self.next_par = 1 - parity if kind != "prologue" else 0
        self.steps = {"prologue": 0, "tail": 0}.get(kind, GI)

    def bank(self, i, job, arg):
        b, n = TABLES[self.kind][0][(i, job, arg)]
        return b, uses_before(self.kind, self.g, b) + n

    def jobs(self, i, slot):
        return [(j, a) for s, j, a in body_jobs(self.kind)[i] if s == slot]

    def finished(self, i, tile_of):
        prev = (tile_of == "wo" and i == 0) or (tile_of == "D" and i <= 1)
        if self.kind == "tail":
            return NG - 1, (NG - 1) % 2, (NG - 1) // 2
        return (self.g - 1, 1 - self.parity, self.earlier_prev) if prev else (self.g, self.parity, self.earlier)


def all_bodies(eng, run):
    run(Body("prologue", 0, 0))
    run(Body("first", 0, 0))
    with eng.Fori(0, (NG - 2) // 2) as pair:
        run(Body("mid", pair * 2 + 1, 1, pair, pair))
        run(Body("mid", pair * 2 + 2, 0, pair + 1, pair))
    run(Body("last", NG - 1, 1))
    run(Body("tail", NG, 0))


def build(nc, xT, wtok, wqk, wv, wo, w1, b1, w2, btok, bqk, bv, bo, wg, bg, b2, rope_cos, rope_sin,
          ident_in, tri_in, ones_in, scan_mask, desc_in, base_in, tokid_in, tvec_in, out):
    rows_d = nc.dram_tensor("token_rows", (NTOK + 1, ROW), F32, kind="Internal").ap()
    parts_d = [nc.dram_tensor(f"parts{f}", (3, 2 * E, HALF), BF16, kind="Internal").ap() for f in range(2)]
    list_d = nc.dram_tensor("expert_lists", (LIST, 1), I32, kind="Internal").ap()

    with ExitStack() as whole:
        def sem(name):
            return whole.enter_context(nc.semaphore(name))

        def sb_in(ctx, name, shape, dt=F32):
            return ctx.enter_context(nc.sbuf_tensor(name, shape, dt))

        def sb(name, shape, dt=F32):
            return sb_in(whole, name, shape, dt)

        w1_sb = sb("w1_sb", [KC + 1, NE, 2, HID])
        w2_sb = sb("w2_sb", [128, NE, PJ, E])
        ident = sb("ident", [128, 128])
        identb = sb("identb", [128, 128], BF16)
        places = sb("places", [TP, NE])
        base_sb = sb("base_sb", [TP, NE])
        tvec = sb("tvec", [1, NFT])
        tile_expert = sb("tile_expert", [1, NFT], I32)
        tile_place = sb("tile_place", [1, NFT], I32)

        loaded = sem("loaded")
        loaded2 = sem("loaded2")
        rows_stored = [sem(f"rows_stored{p}") for p in range(2)]
        filled = sem("filled")
        listed = [sem(f"listed{p}") for p in range(2)]
        consts_set = sem("consts_set")

        waits_passed = sem("waits_passed")

        def settle(eng):
            eng.sem_inc(waits_passed, 1)

        with ExitStack() as ctx:
            def s1(name, shape, dt=F32):
                return sb_in(ctx, name, shape, dt)

            wtok_sb = s1("wtok_sb", [128, PJ, E])
            wqk_sb = s1("wqk_sb", [KC, 2, 2 * E])
            wv_sb = s1("wv_sb", [KC, 2, E])
            wo_sb = s1("wo_sb", [KC, 2, E])
            btok_sb = s1("btok_sb", [TP, E])
            bqk_sb = s1("bqk_sb", [TP, 2 * E])
            bv_sb = s1("bv_sb", [QC, E])
            bo_sb = s1("bo_sb", [TP, E])
            wg_sb = s1("wg_sb", [TP, NE, E])
            bg_sb = s1("bg_sb", [TP, NE])
            cos_sb = s1("cos_sb", [TP, NT, 2, 4])
            sin_sb = s1("sin_sb", [TP, NT, 2, 4])
            tri = s1("tri", [TP, TP])
            ones = s1("ones", [TP, TP])
            mask_sb = s1("mask_sb", [TP, NE * NT])
            desc_sb = s1("desc_sb", [TP, NE])
            tok_now = s1("tok_now", [TP, 2, NT], I32)
            half_neg = s1("half_neg", [TP, 1])
            sentinels = s1("sentinels", [128, LIST // 128 // FILLS], I32)
            nowhere = s1("nowhere", [TP, 1], I32)
            zero_row = s1("zero_row", [1, ROW])

            x_sb = s1("x_sb", [128, NT, PJ, TP])
            h = s1("h", [TP, 2, NT, E])
            stats = s1("stats", [TP, 2, 6])
            mv = s1("mv", [TP, 2, 2])
            rstd = s1("rstd", [TP, 2, 1])
            hn = s1("hn", [TP, 2, E])
            hnT = s1("hnT", [KC, 2, GT])
            qk = s1("qk", [TP, 2, 2 * E])
            rot = s1("rot", [TP, 2 * NH, 2, 4])
            qkT = s1("qkT", [KC, 4, TP])
            parts = [s1(f"part{n}", [KC, 4, GT], BF16) for n in range(3)]
            qst = s1("qst", [SK + 2, NH, GT], BF16)
            kst = s1("kst", [SK + 2, NH, GT], BF16)
            v_sb = s1("v_sb", [QC, 2, 2 * GI, NH, HD + 1])
            nmax = s1("nmax", [QC, 2, NH])
            nrest = s1("nrest", [QC, 2, NH])
            nparts = s1("nparts", [QC, 2, 2 * NH], BF16)
            nT = s1("nT", [2 * NH, TOK], BF16)
            prob = s1("prob", [QC, 4, 2, TOK])
            oT = s1("oT", [128, 3, TOK])
            rden = s1("rden", [QC, 2, NH])
            on = s1("on", [QC, 2, E])
            onT = s1("onT", [KC, 2, GT])
            h2 = s1("h2", [TP, 2, NT, ROW])
            stats2 = s1("stats2", [TP, 2, 6])
            hn2 = s1("hn2", [TP, E])
            junk = s1("junk", [TP, NE, E])
            logit = s1("logit", [TP, NE, NT])
            top = s1("top", [TP, NT])
            pick = s1("pick", [TP, NE, NT])
            hot = s1("hot", [TP, NE, NT])
            seen = s1("seen", [TP, NE, NT])
            start = s1("start", [TP, NE])
            place = s1("place", [TP, NE, NT])
            place1 = s1("place1", [TP, NT])
            place_i = s1("place_i", [TP, 2, NT], I32)

            s_bank = [ctx.enter_context(nc.psum_tensor(f"s_bank{n}", [128, 512], F32)) for n in range(2)]
            st_bank = [ctx.enter_context(nc.psum_tensor(f"st_bank{n}", [128, 512], F32)) for n in range(2)]
            o_bank = ctx.enter_context(nc.psum_tensor("o_bank", [128, 512], F32))
            work = [ctx.enter_context(nc.psum_tensor(f"work{n}", [128, 512], F32)) for n in range(WORK_BANKS)]

            work_written = [sem(f"work_written{n}") for n in range(WORK_BANKS)]
            work_read = [sem(f"work_read{n}") for n in range(WORK_BANKS)]
            x_in = [sem(f"x_in{t}") for t in range(NT)]
            stats_made = sem("stats_made")
            mv_made = sem("mv_made")
            eps_added = sem("eps_added")
            rstd_made = sem("rstd_made")
            hn_made = sem("hn_made")
            bo_added = sem("bo_added")
            rope_step = sem("rope_step")
            roped = sem("roped")
            split_step = sem("split_step")
            split_made = sem("split_made")
            parts_out = [sem(f"parts_out{f}") for f in range(2)]
            stacked = [sem(f"stacked{f}") for f in range(2)]
            s_written = sem("s_written")
            max_made = sem("max_made")
            nmax_step = sem("nmax_step")
            nparts_made = sem("nparts_made")
            shifted = sem("shifted")
            st_written = sem("st_written")
            exp_made = sem("exp_made")
            pv_written = sem("pv_written")
            o_read = sem("o_read")
            rden_made = sem("rden_made")
            h2_made = sem("h2_made")
            stats2_made = sem("stats2_made")
            mv2_made = sem("mv2_made")
            eps2_added = sem("eps2_added")
            rstd2_made = sem("rstd2_made")
            hn2_made = sem("hn2_made")
            logit_made = sem("logit_made")
            route_step = sem("route_step")
            seen_made = sem("seen_made")
            placed = sem("placed")
            o_cleared = sem("o_cleared")

            STACK_INC = 16 * 2 * NSPLIT
            ROUTE_STEPS = 11

            block = ctx.enter_context(nc.Block())

            @block.sync
            def _(sp):
                def load_x(group, t):
                    if isinstance(group, int):
                        src = xT[group * NT + t]
                    else:
                        src = xT.rearrange("(g t) p n -> g t p n", t=NT)[bass.ds(group, 1), t, :, :].rearrange(
                            "g p n -> (g p) n")
                    sp.dma_start(x_sb[:, t, :, :].rearrange("p j n -> p (j n)"), src).then_inc(x_in[t], 16)

                for t in range(2):
                    load_x(0, t)
                consts = [(wtok_sb, wtok), (btok_sb, btok), (ident, ident_in), (wqk_sb, wqk), (bqk_sb, bqk),
                          (cos_sb, rope_cos), (sin_sb, rope_sin), (wv_sb, wv), (bv_sb, bv), (wo_sb, wo),
                          (bo_sb, bo), (wg_sb, wg), (bg_sb, bg), (tri, tri_in), (ones, ones_in),
                          (mask_sb, scan_mask), (desc_sb, desc_in), (base_sb, base_in), (places, base_in),
                          (tok_now[:, 1, :], tokid_in), (tvec, tvec_in)]
                for dst, src in consts:
                    d = dst if isinstance(dst, bass.AP) else dst[tuple([slice(None)] * len(dst.shape))]
                    sp.dma_start(d, src).then_inc(loaded, 16)
                assert len(consts) == N_CONSTS
                for t in range(2, NT):
                    load_x(0, t)
                sp.dma_start(w1_sb[0:KC], w1).then_inc(loaded2, 16)
                sp.dma_start(w1_sb[KC:KC + 1, :, 1, :], b1).then_inc(loaded2, 16)
                sp.dma_start(w2_sb[:], w2).then_inc(loaded2, 16)
                sp.wait_ge(consts_set, 7)
                for f in range(FILLS):
                    sp.dma_start(list_d.rearrange("(f p n) o -> f p (n o)", f=FILLS, p=128)[f],
                                 sentinels[:]).then_inc(filled if f else rows_stored[0], 16)
                sp.wait_ge(filled, 16 * (FILLS - 1))
                sp.dma_start(rows_d[NTOK:NTOK + 1, :], zero_row[:]).then_inc(rows_stored[1], 16)

                def stack(group, f):
                    wait(sp, split_made, group * NT + (4 if f == 0 else 7))
                    settle(sp)
                    wait(sp, st_written, (group * GI + 2 * f - 2) * NH)
                    settle(sp)
                    cols = slice(f * HALF, (f + 1) * HALF)
                    wait(sp, stacked[f], group * STACK_INC)
                    for which in range(3):
                        sp.dma_start(parts_d[f][which].rearrange("(c p) t -> p c t", c=4),
                                     parts[which][:, :, cols]).then_inc(parts_out[f], 16)
                    sp.wait_ge(parts_out[f], (group + 1) * 48)
                    for n in range(NSPLIT):
                        for dst, a, which in ((qst, 0, Q_PARTS[n]), (kst, E, K_PARTS[n])):
                            sp.dma_start(dst[n * HD:(n + 1) * HD, :, cols],
                                         parts_d[f][which, a:a + E].rearrange("(h d) t -> d h t", d=HD)
                                         ).then_inc(stacked[f], 16)

                def shift(i, step):
                    b, n = step
                    sp.wait_ge(work_read[b], n + 1)
                    for s in range(2):
                        sp.dma_start(qst[SK + s:SK + s + 1, :, i * TOK:(i + 1) * TOK],
                                     nT[s * NH:(s + 1) * NH, :]
                                     ).then_inc(shifted, 16)

                def run(bd):
                    g = bd.g
                    if bd.kind == "prologue":
                        for t in range(NT):
                            load_next(bd, 0, t)
                        stack(0, 0)
                        shift(0, bd.bank(1, "trM", 0))
                        return
                    if bd.kind == "tail":
                        store_rows(NG - 1, (NG - 1) % 2)
                        return
                    for i in range(GI):
                        if i == 0:
                            stack(g, 1)
                        if i == 2 and bd.kind != "last":
                            stack(g + 1, 0)
                        if i == 2 and bd.kind != "first":
                            store_rows(g - 1, 1 - bd.parity)
                        for t in A_TILES[i]:
                            if bd.kind == "last":
                                break
                            if isinstance(g, int) and g + 2 >= NG:
                                break
                            load_next(bd, i, t)
                        if not (bd.kind == "last" and i == 3):
                            shift((i + 1) % GI, bd.bank(i, "trM", 0))

                def load_next(bd, i, t):
                    b, n = bd.bank(i, "patch", t)
                    sp.wait_ge(work_read[b], n + 1)
                    load_x(bd.next + 1, t)

                def store_rows(group, par):
                    sp.wait_ge(rstd2_made, group * NT + NT)
                    dst = (rows_d[0:NTOK].rearrange("(g t p) c -> g p t c", t=NT, p=TP)[group]
                           if isinstance(group, int) else
                           rows_d[0:NTOK].rearrange("(g t p) c -> g p t c", t=NT, p=TP)[bass.ds(group, 1)]
                           .rearrange("g p t c -> (g p) t c"))
                    sp.dma_start(dst, h2[:, par, :, :]).then_inc(rows_stored[par], 16)

                run(Body("prologue", 0, 0))
                run(Body("first", 0, 0))
                with sp.Fori(0, (NG - 2) // 2 - 1) as pair:
                    run(Body("mid", pair * 2 + 1, 1, pair, pair))
                    run(Body("mid", pair * 2 + 2, 0, pair + 1, pair))
                run(Body("mid", NG - 3, 1))
                run(Body("mid", NG - 2, 0))
                run(Body("last", NG - 1, 1))
                run(Body("tail", NG, 0))
                sp.wait_ge(rows_stored[0], 16 * (NG // 2 + 1))
                sp.wait_ge(rows_stored[1], 16 * (NG // 2 + 1))
                sp.wait_ge(loaded2, 48)

            @block.tensor
            def _(pe):
                def wait_read(bd, i, job, arg):
                    b, n = bd.bank(i, job, arg)
                    pe.wait_ge(work_read[b], n + 1)

                def begin(bd, i, job, arg):
                    b, n = bd.bank(i, job, arg)
                    wait(pe, work_read[b], n)
                    return work[b], work_written[b]

                def patch(bd, i, t):
                    bank, written = begin(bd, i, "patch", t)
                    pe.wait_ge(x_in[t], (bd.next + 1) * 16)
                    for j in range(PJ):
                        mm = pe.matmul(bank[0:TP, 0:E], x_sb[:, t, j, :], wtok_sb[:, j, :],
                                       start=(j == 0), stop=(j == PJ - 1))
                    mm.then_inc(written, 1)

                def trH(bd, i, t):
                    T = bd.next * NT + t
                    bank, written = begin(bd, i, "trH", t)
                    pe.wait_ge(hn_made, T + 1)
                    tp = (bd.next_par + t) % 2
                    for c in range(2):
                        mm = pe.transpose(bank[0:KC, c * TP:(c + 1) * TP], hn[:, tp, c * KC:(c + 1) * KC],
                                          ident[0:TP, 0:TP])
                    mm.then_inc(written, 1)

                def qk_product(bd, i, t):
                    bank, written = begin(bd, i, "qk", t)
                    wait_read(bd, i, "trH", t)
                    for c in range(2):
                        mm = pe.matmul(bank[0:TP, 0:2 * E], hnT[:, c, t * TP:(t + 1) * TP], wqk_sb[:, c, :],
                                       start=(c == 0), stop=(c == 1))
                    mm.then_inc(written, 1)

                def trQ(bd, i, t):
                    T = bd.next * NT + t
                    bank, written = begin(bd, i, "trQ", t)
                    pe.wait_ge(roped, T + 1)
                    tp = (bd.next_par + t) % 2
                    for c in range(4):
                        mm = pe.transpose(bank[0:KC, c * TP:(c + 1) * TP], qk[:, tp, c * KC:(c + 1) * KC],
                                          ident[0:TP, 0:TP])
                    mm.then_inc(written, 1)

                def v_product(bd, i, m):
                    bank, written = begin(bd, i, "V", m)
                    wait_read(bd, i, "trH", NT - 1)
                    for k in range(2):
                        for c in range(2):
                            a = (2 * m + k) * QC
                            mm = pe.matmul(bank[0:QC, k * E:(k + 1) * E], hnT[:, c, a:a + QC], wv_sb[:, c, :],
                                           start=(c == 0), stop=(c == 1))
                    mm.then_inc(written, 1)

                def trO(bd, i, c, image):
                    bank, written = begin(bd, i, "trO", c)
                    pe.wait_ge(o_read, (image + 1) * 3)
                    for q in range(3):
                        mm = pe.transpose(bank[0:QC, q * 128:(q + 1) * 128], oT[:, q, c * QC:(c + 1) * QC],
                                          ident[:, :])
                    mm.then_inc(written, 1)

                def trN(bd, i, image):
                    bank, written = begin(bd, i, "trN", 0)
                    wait_read(bd, i, "trO", 1)
                    for c in range(2):
                        for k in range(2):
                            mm = pe.transpose(bank[0:KC, c * TOK + k * QC:c * TOK + (k + 1) * QC],
                                              on[:, k, c * KC:(c + 1) * KC], ident[0:QC, 0:QC])
                    mm.then_inc(written, 1)

                def wo_product(bd, i, tiles, image):
                    bank, written = begin(bd, i, "wo", tiles)
                    wait_read(bd, i, "trN", 0)
                    for n, t in enumerate(tiles):
                        for c in range(2):
                            mm = pe.matmul(bank[0:TP, n * E:(n + 1) * E], onT[:, c, t * TP:(t + 1) * TP],
                                           wo_sb[:, c, :], start=(c == 0), stop=(c == 1))
                    mm.then_inc(written, 1)

                def trM(bd, i, image):
                    bank, written = begin(bd, i, "trM", 0)
                    pe.wait_ge(nparts_made, image + 1)
                    narrow = bank[:, :].bitcast(BF16)
                    for k in range(2):
                        mm = pe.transpose(narrow[0:2 * NH, k * QC:(k + 1) * QC],
                                          nparts[:, k, :], identb[0:QC, 0:QC])
                    mm.then_inc(written, 1)

                def route(bd, i, group):
                    bank, written = begin(bd, i, "route", 0)
                    pe.wait_ge(seen_made, group + 1)
                    pe.matmul(bank[0:TP, 0:NE], tri[:, :], seen[:, :, NT - 1], start=True, stop=True)
                    pe.matmul(bank[0:TP, NE:2 * NE], ones[:, :], seen[:, :, NT - 1], start=True,
                              stop=True).then_inc(written, 1)

                def scores(image, i, hd):
                    if hd == 0:
                        f = (i % GI) // 2
                        group = image // GI if isinstance(image, int) else image_group(image, i)
                        pe.wait_ge(stacked[f], (group + 1) * STACK_INC)
                    H = image * NH + hd
                    wait(pe, max_made, H - 1)
                    a = (i % GI) * TOK
                    for k in range(2):
                        mm = pe.matmul(s_bank[hd % 2][0:QC, k * TOK:(k + 1) * TOK],
                                       qst[0:SK, hd, a + k * QC:a + (k + 1) * QC], kst[0:SK, hd, a:a + TOK],
                                       start=True, stop=True)
                    mm.then_inc(s_written, 1)

                def image_group(image, i):
                    return groups_at[0] + (1 if i == GI else 0)

                groups_at = [0]

                def scores_T(image, i, hd):
                    if hd == 0:
                        pe.wait_ge(shifted, (image + 1) * 32)
                    H = image * NH + hd
                    wait(pe, exp_made, H - 1)
                    a = i * TOK
                    for k in range(2):
                        mm = pe.matmul(st_bank[hd % 2][0:QC, k * TOK:(k + 1) * TOK],
                                       kst[:, hd, a + k * QC:a + (k + 1) * QC], qst[:, hd, a:a + TOK],
                                       start=True, stop=True)
                    mm.then_inc(st_written, 1)

                def pv(image, i, par, hd):
                    H = image * NH + hd
                    pe.wait_ge(exp_made, H + 1)
                    if hd % 4 == 0:
                        wait(pe, o_read, image * 3 + hd // 4)
                    q = hd % 4
                    for k in range(2):
                        mm = pe.matmul(o_bank[32 * q:32 * q + HD + 1, 0:TOK], v_sb[:, par, 2 * i + k, hd, :],
                                       prob[:, hd % 4, k, :], start=(k == 0), stop=(k == 1),
                                       tile_position=(0, 32 * q))
                    mm.then_inc(pv_written, 1)

                def do_jobs(bd, i, slot, image):
                    for job, arg in bd.jobs(i, slot):
                        if job == "patch":
                            patch(bd, i, arg)
                        elif job == "trH":
                            trH(bd, i, arg)
                        elif job == "qk":
                            qk_product(bd, i, arg)
                        elif job == "trQ":
                            trQ(bd, i, arg)
                        elif job == "V":
                            v_product(bd, i, arg)
                        elif job == "trO":
                            trO(bd, i, arg, image - 1)
                        elif job == "trN":
                            trN(bd, i, image - 1)
                        elif job == "wo":
                            wo_product(bd, i, arg, image - 1)
                        elif job == "trM":
                            trM(bd, i, image + 1)
                        elif job == "route":
                            route(bd, i, bd.finished(i, "D")[0])

                def run(bd):
                    groups_at[0] = bd.g
                    if bd.kind == "prologue":
                        do_jobs(bd, 0, 0, 0)
                        for hd in range(NH):
                            scores(0, 0, hd)
                        do_jobs(bd, 1, 1, -1)
                        return
                    if bd.kind == "tail":
                        for hd in (NH - 2, NH - 1):
                            pv(B - 1, GI - 1, (NG - 1) % 2, hd)
                        for i in range(2):
                            for slot in range(NH):
                                do_jobs(bd, i, slot, B)
                        return
                    for i in range(GI):
                        image = bd.g * GI + i
                        for slot in range(NH):
                            if not (bd.kind == "last" and i == GI - 1):
                                for hd in S_HEADS[slot]:
                                    scores(image + 1, i + 1, hd)
                            scores_T(image, i, slot)
                            do_jobs(bd, i, slot, image)
                            if slot >= 2:
                                pv(image, i, bd.parity, slot - 2)
                            elif not (bd.kind == "first" and i == 0):
                                pv(image - 1, (i - 1) % GI, bd.parity if i else 1 - bd.parity, NH - 2 + slot)

                pe.wait_ge(loaded, 16 * N_CONSTS)
                pe.wait_ge(consts_set, 7)
                pe.wait_ge(o_cleared, 1)
                all_bodies(pe, run)

            @block.scalar
            def _(act):
                def copy(out_, in_):
                    return act.activation(out_, in_, ACT.Copy)

                def do_jobs(bd, i, slot, image):
                    for job, arg in bd.jobs(i, slot):
                        if job not in ("trH", "trQ", "trN", "trM"):
                            continue
                        b, n = bd.bank(i, job, arg)
                        act.wait_ge(work_written[b], n + 1)
                        bank, read = work[b], work_read[b]
                        if job == "trH":
                            ins = copy(hnT[:, :, arg * TP:(arg + 1) * TP],
                                       bank[0:KC, 0:2 * TP].rearrange("p (c t) -> p c t", c=2))
                            ins.then_inc(read, 1)
                        elif job == "trQ":
                            T = bd.next * NT + arg
                            wait(act, split_made, T)
                            wait(act, parts_out[0 if arg < 3 else 1], bd.next * 48)
                            if arg == 3:
                                wait(act, parts_out[0], bd.next * 48)
                            view = bank[0:KC, 0:4 * TP].rearrange("p (c t) -> p c t", c=4)
                            copy(qkT[:, :, :], view)
                            copy(parts[0][:, :, arg * TP:(arg + 1) * TP], view).then_inc(read, 1)
                        elif job == "trN":
                            a = ((i - 1) % GI) * TOK
                            copy(onT[:, :, a:a + TOK],
                                 bank[0:KC, 0:2 * TOK].rearrange("p (c t) -> p c t", c=2)).then_inc(read, 1)
                        else:
                            wait(act, shifted, (image + 1) * 32)
                            copy(nT[:, :], bank[:, :].bitcast(BF16)[0:2 * NH, 0:TOK]).then_inc(read, 1)

                def read_o(image, q, before=None):
                    act.wait_ge(pv_written, image * NH + 4 * q + 4)
                    if before is not None:
                        b, n = before
                        act.wait_ge(work_written[b], n + 1)
                    copy(oT[:, q, :], o_bank[:, 0:TOK]).then_inc(o_read, 1)

                def run(bd):
                    if bd.kind == "prologue":
                        do_jobs(bd, 0, 0, 0)
                        do_jobs(bd, 1, 1, -1)
                        return
                    if bd.kind == "tail":
                        read_o(B - 1, 2)
                        for i in range(2):
                            for slot in range(NH):
                                do_jobs(bd, i, slot, B)
                        return
                    for i in range(GI):
                        image = bd.g * GI + i
                        start_up = bd.kind == "first" and i == 0
                        for slot in range(NH):
                            if slot == 2 and not start_up:
                                read_o(image - 1, 2)
                            if slot == 6:
                                read_o(image, 0, None if start_up else bd.bank(i, "trO", 1))
                            if slot == 10:
                                read_o(image, 1)
                            H = image * NH + slot
                            act.wait_ge(st_written, H + 1)
                            wait(act, pv_written, H - 3)
                            act.activation(prob[:, slot % 4, :, :],
                                           st_bank[slot % 2][0:QC, 0:2 * TOK].rearrange("p (k t) -> p k t", k=2),
                                           ACT.Exp, scale=float(HD) ** -0.5).then_inc(exp_made, 1)
                            do_jobs(bd, i, slot, image)

                all_bodies(act, run)

            @block.vector
            def _(dve):
                def chain(ins, s, value):
                    ins.then_inc(s, 1)
                    dve.wait_ge(s, value)

                def reader(bd, i, job, arg):
                    b, n = bd.bank(i, job, arg)
                    dve.wait_ge(work_written[b], n + 1)
                    return work[b], work_read[b], n

                def patch(bd, i, t):
                    T = bd.next * NT + t
                    par, tp = bd.next_par, (bd.next_par + t) % 2
                    bank, read, n = reader(bd, i, "patch", t)
                    dve.tensor_tensor(h[:, par, t, :], bank[0:TP, 0:E], btok_sb[:, :], ALU.add).then_inc(read, 1)
                    dve.wait_ge(read, n + 1)
                    chain(dve.bn_stats(stats[:, tp, :], h[:, par, t, :]), stats_made, T + 1)
                    settle(dve)
                    dve.bn_aggr(mv[:, tp, :], stats[:, tp, :]).then_inc(mv_made, 1)

                def norm(bd, t):
                    T = bd.next * NT + t
                    par, tp = bd.next_par, (bd.next_par + t) % 2
                    dve.wait_ge(rstd_made, T + 1)
                    dve.tensor_scalar(hn[:, tp, :], h[:, par, t, :], mv[:, tp, 0:1], rstd[:, tp, 0:1],
                                      ALU.subtract, ALU.mult).then_inc(hn_made, 1)

                def qk_bias(bd, i, t):
                    T = bd.next * NT + t
                    bank, read, n = reader(bd, i, "qk", t)
                    wait(dve, split_made, T - 1)
                    dve.tensor_tensor(qk[:, (bd.next_par + t) % 2, :], bank[0:TP, 0:2 * E], bqk_sb[:, :],
                                      ALU.add).then_inc(read, 1)

                def v_bias(bd, i, m):
                    bank, read, n = reader(bd, i, "V", m)
                    wait(dve, pv_written, (bd.next - 1) * GI * NH)
                    for k in range(2):
                        ins = dve.tensor_tensor(
                            v_sb[:, bd.next_par, 2 * m + k, :, 0:HD],
                            bank[0:QC, k * E:(k + 1) * E].rearrange("p (h d) -> p h d", d=HD),
                            bv_sb[:, :].rearrange("p (h d) -> p h d", d=HD), ALU.add)
                    ins.then_inc(read, 1)

                def divide(bd, i, c, image):
                    bank, read, n = reader(bd, i, "trO", c)
                    view = bank[0:QC, 0:3 * 128].rearrange("p (h d) -> p h d", d=32)
                    chain(dve.reciprocal(rden[:, c, :], view[:, :, HD]), rden_made, 2 * image + c + 1)
                    dve.tensor_tensor(on[:, c, :].rearrange("p (h d) -> p h d", d=HD), view[:, :, 0:HD],
                                      rden[:, c, :].unsqueeze(2).to_broadcast([QC, NH, HD]),
                                      ALU.mult).then_inc(read, 1)

                def residual(bd, i, tiles):
                    group, par, earlier = bd.finished(i, "wo")
                    bank, read, n = reader(bd, i, "wo", tiles)
                    wait(dve, bo_added, group * NT + tiles[-1] + 1)
                    dve.wait_ge(rows_stored[par], 16 * (earlier + 1))
                    m = len(tiles)
                    dve.tensor_tensor(h2[:, par, tiles[0]:tiles[0] + m, 0:E],
                                      bank[0:TP, 0:m * E].rearrange("p (t c) -> p t c", t=m),
                                      h[:, par, tiles[0]:tiles[0] + m, :], ALU.add).then_inc(read, 1)
                    dve.wait_ge(read, n + 1)
                    for t in tiles:
                        T = group * NT + t
                        chain(dve.bn_stats(stats2[:, t % 2, :], h2[:, par, t, 0:E]), stats2_made, T + 1)
                        settle(dve)
                        dve.bn_aggr(h2[:, par, t, E:E + 2], stats2[:, t % 2, :]).then_inc(mv2_made, 1)

                def logits(bd, i, t):
                    group, par, _ = bd.finished(i, "D")
                    T = group * NT + t
                    dve.wait_ge(rstd2_made, T + 1)
                    wait(dve, logit_made, T)
                    chain(dve.tensor_scalar(hn2[:, :], h2[:, par, t, 0:E], h2[:, par, t, E:E + 1],
                                            h2[:, par, t, E + 1:E + 2], ALU.subtract, ALU.mult), hn2_made, T + 1)
                    for e in range(NE):
                        ins = dve.tensor_tensor_reduce(junk[:, e, :], hn2[:, :], wg_sb[:, e, :], 1.0, 0.0, ALU.mult,
                                                       ALU.add, logit[:, e, t:t + 1])
                    ins.then_inc(logit_made, 1)

                def route(bd, i):
                    group, par, earlier = bd.finished(i, "D")
                    n = [0]

                    def step(ins):
                        n[0] += 1
                        chain(ins, route_step, group * ROUTE_STEPS + n[0])

                    def over_tiles(a):
                        return a.unsqueeze(2).to_broadcast([TP, NE, NT])

                    def over_experts(a):
                        return a.unsqueeze(1).to_broadcast([TP, NE, NT])

                    dve.wait_ge(logit_made, group * NT + NT)
                    step(dve.tensor_tensor(logit[:, :, :], logit[:, :, :], over_tiles(bg_sb[:, :]), ALU.add))
                    step(dve.tensor_reduce(top[:, :], logit[:, :, :].rearrange("p e t -> p t e"), AX.X, ALU.max))
                    step(dve.tensor_tensor(pick[:, :, :], logit[:, :, :], over_experts(top[:, :]), ALU.is_ge))
                    step(dve.tensor_tensor(pick[:, :, :], pick[:, :, :], over_tiles(desc_sb[:, :]), ALU.mult))
                    step(dve.tensor_reduce(top[:, :], pick[:, :, :].rearrange("p e t -> p t e"), AX.X, ALU.max))
                    step(dve.tensor_tensor(hot[:, :, :], pick[:, :, :], over_experts(top[:, :]), ALU.is_equal))
                    dve.tensor_tensor_scan(seen[:, :, :].rearrange("p e t -> p (e t)"), mask_sb[:, :],
                                           hot[:, :, :].rearrange("p e t -> p (e t)"), 0.0, ALU.mult,
                                           ALU.add).then_inc(seen_made, 1)
                    bank, read, m = reader(bd, i, "route", 0)
                    step(dve.tensor_tensor(start[:, :], bank[0:TP, 0:NE], places[:, :], ALU.add))
                    dve.tensor_tensor(places[:, :], bank[0:TP, NE:2 * NE], places[:, :], ALU.add).then_inc(read, 1)
                    dve.wait_ge(read, m + 1)
                    step(dve.tensor_tensor(place[:, :, :], seen[:, :, :], over_tiles(start[:, :]), ALU.add))
                    step(dve.tensor_tensor(place[:, :, :], place[:, :, :], hot[:, :, :], ALU.mult))
                    step(dve.tensor_reduce(place1[:, :], place[:, :, :].rearrange("p e t -> p t e"), AX.X, ALU.add))
                    dve.wait_ge(listed[par], earlier * (16 * NT) + 16)
                    step(dve.tensor_scalar(tok_now[:, par, :], tok_now[:, 1 - par, :], float(GT), None, ALU.add))
                    dve.tensor_copy(place_i[:, par, :], place1[:, :]).then_inc(placed, 1)
                    assert n[0] == ROUTE_STEPS

                def row_max(image, hd):
                    H = image * NH + hd
                    dve.wait_ge(s_written, H + 1)
                    if hd == 0:
                        wait(dve, nparts_made, image)
                    dve.tensor_reduce(nmax[:, :, hd], s_bank[hd % 2][0:QC, 0:2 * TOK].rearrange(
                        "p (k t) -> p k t", k=2), AX.X, ALU.max, negate=True).then_inc(max_made, 1)

                def split_max(image):
                    dve.wait_ge(max_made, (image + 1) * NH)
                    wait(dve, shifted, image * 32)
                    chain(dve.tensor_copy(nparts[:, :, 0:NH], nmax[:, :, :]), nmax_step, 2 * image + 1)
                    chain(dve.tensor_tensor(nrest[:, :, :], nmax[:, :, :], nparts[:, :, 0:NH], ALU.subtract),
                          nmax_step, 2 * image + 2)
                    dve.tensor_copy(nparts[:, :, NH:2 * NH], nrest[:, :, :]).then_inc(nparts_made, 1)

                def do_jobs(bd, i, slot, image):
                    for job, arg in bd.jobs(i, slot):
                        if job == "patch":
                            patch(bd, i, arg)
                        elif job == "norm":
                            norm(bd, arg)
                        elif job == "qk":
                            qk_bias(bd, i, arg)
                        elif job == "V":
                            v_bias(bd, i, arg)
                        elif job == "trO":
                            divide(bd, i, arg, image - 1)
                        elif job == "wo":
                            residual(bd, i, arg)
                        elif job == "D":
                            logits(bd, i, arg)
                        elif job == "route":
                            route(bd, i)
                        elif job == "negmax":
                            split_max(image + 1)

                def run(bd):
                    if bd.kind == "prologue":
                        do_jobs(bd, 0, 0, 0)
                        for hd in range(NH):
                            row_max(0, hd)
                        do_jobs(bd, 1, 0, -1)
                        return
                    if bd.kind == "tail":
                        for i in range(2):
                            for slot in range(NH):
                                do_jobs(bd, i, slot, B)
                        return
                    for i in range(GI):
                        image = bd.g * GI + i
                        for slot in range(NH):
                            if not (bd.kind == "last" and i == GI - 1):
                                for hd in S_HEADS[slot]:
                                    row_max(image + 1, hd)
                            do_jobs(bd, i, slot, image)

                dve.memset(o_bank[:, :], 0.0).then_inc(o_cleared, 1)
                dve.memset(kst[SK:SK + 2, :, :], 1.0).then_inc(consts_set, 1)
                dve.memset(v_sb[:, :, :, :, HD:HD + 1].rearrange("p a b h o -> p (a b h) o"), 1.0).then_inc(consts_set, 1)
                dve.wait_ge(loaded, 16 * N_CONSTS)
                dve.tensor_copy(identb[:, :], ident[:, :]).then_inc(consts_set, 1)
                all_bodies(dve, run)

            @block.gpsimd
            def _(pool):
                def power(dst, count_wait, s_eps, s_done, T):
                    count_wait()
                    settle(pool)
                    pool.tensor_scalar(dst[0], dst[1], EPS, None, ALU.add).then_inc(s_eps, 1)
                    pool.wait_ge(s_eps, T + 1)
                    pool.tensor_tensor(dst[0], dst[0], half_neg[:, 0:1], ALU.pow).then_inc(s_done, 1)

                def patch(bd, t):
                    T = bd.next * NT + t
                    tp = (bd.next_par + t) % 2

                    def ready():
                        pool.wait_ge(mv_made, T + 1)
                        wait(pool, hn_made, T - 1)
                    power((rstd[:, tp, :], mv[:, tp, 1:2]), ready, eps_added, rstd_made, T)

                def add_bo(bd, t):
                    T = bd.next * NT + t
                    pool.wait_ge(hn_made, T + 1)
                    pool.tensor_tensor(h[:, bd.next_par, t, :], h[:, bd.next_par, t, :], bo_sb[:, :],
                                       ALU.add).then_inc(bo_added, 1)

                def rope(bd, i, t):
                    T = bd.next * NT + t
                    b, n = bd.bank(i, "qk", t)
                    pool.wait_ge(work_read[b], n + 1)
                    view = qk[:, (bd.next_par + t) % 2, :].rearrange("p (h a d) -> p h a d", a=2, d=HD // 2)
                    first = view[:, :, :, 0:4]

                    def table(x):
                        return x[:, t, :, :].unsqueeze(1).to_broadcast([TP, 2 * NH, 2, 4])

                    wait(pool, roped, T)
                    pool.tensor_tensor(rot[:, :, :, :], first, table(sin_sb), ALU.mult).then_inc(rope_step, 1)
                    pool.wait_ge(rope_step, 3 * T + 1)
                    pool.tensor_tensor(first, first, table(cos_sb), ALU.mult).then_inc(rope_step, 1)
                    pool.wait_ge(rope_step, 3 * T + 2)
                    pool.tensor_tensor(first[:, :, 0, :], first[:, :, 0, :], rot[:, :, 1, :],
                                       ALU.add).then_inc(rope_step, 1)
                    pool.wait_ge(rope_step, 3 * T + 3)
                    pool.tensor_tensor(first[:, :, 1, :], first[:, :, 1, :], rot[:, :, 0, :],
                                       ALU.add).then_inc(roped, 1)

                def split(bd, i, t):
                    T = bd.next * NT + t
                    cols = slice(t * TP, (t + 1) * TP)
                    b, n = bd.bank(i, "trQ", t)
                    pool.wait_ge(work_read[b], n + 1)
                    pool.tensor_tensor(qkT[:, :, :], qkT[:, :, :], parts[0][:, :, cols],
                                       ALU.subtract).then_inc(split_step, 1)
                    pool.wait_ge(split_step, 2 * T + 1)
                    settle(pool)
                    pool.tensor_copy(parts[1][:, :, cols], qkT[:, :, :]).then_inc(split_step, 1)
                    pool.wait_ge(split_step, 2 * T + 2)
                    pool.tensor_tensor(parts[2][:, :, cols], qkT[:, :, :], parts[1][:, :, cols],
                                       ALU.subtract).then_inc(split_made, 1)

                def statistics2(bd, i, tiles):
                    group, par, _ = bd.finished(i, "wo")
                    for t in tiles:
                        T = group * NT + t
                        var = h2[:, par, t, E + 1:E + 2]
                        power((var, var), lambda: pool.wait_ge(mv2_made, T + 1), eps2_added, rstd2_made, T)

                def list_tokens(bd, i):
                    group, par, _ = bd.finished(i, "D")
                    pool.wait_ge(placed, group + 1)
                    settle(pool)
                    for t in range(NT):
                        pool.indirect_dma_start(
                            out=list_d, out_offset=bass.IndirectOffsetOnAxis(
                                ap=place_i[:, par, t:t + 1].bitcast(U32), axis=0),
                            in_=tok_now[:, par, t:t + 1], in_offset=None, bounds_check=LIST - 1,
                            oob_is_err=False).then_inc(listed[par], 16)

                def do_jobs(bd, i, slot):
                    for job, arg in bd.jobs(i, slot):
                        if job == "patch":
                            patch(bd, arg)
                        elif job == "norm":
                            add_bo(bd, arg)
                        elif job == "qk":
                            rope(bd, i, arg)
                        elif job == "trQ":
                            split(bd, i, arg)
                        elif job == "wo":
                            statistics2(bd, i, arg)
                        elif job == "route":
                            list_tokens(bd, i)

                def run(bd):
                    for i in range(len(body_jobs(bd.kind))):
                        for slot in range(NH):
                            do_jobs(bd, i, slot)

                pool.memset(half_neg[:, :], -0.5).then_inc(consts_set, 1)
                pool.memset(zero_row[:, :], 0.0).then_inc(consts_set, 1)
                pool.memset(nowhere[:, :], LIST).then_inc(consts_set, 1)
                pool.memset(sentinels[:, :], NTOK).then_inc(consts_set, 1)
                pool.wait_ge(loaded, 16 * N_CONSTS)
                pool.wait_ge(consts_set, 7)
                for par in range(2):
                    pool.indirect_dma_start(
                        out=list_d, out_offset=bass.IndirectOffsetOnAxis(ap=nowhere[:, :].bitcast(U32), axis=0),
                        in_=nowhere[:, :], in_offset=None, bounds_check=LIST - 1,
                        oob_is_err=False).then_inc(listed[par], 16)
                pool.wait_ge(rows_stored[0], 16)
                pool.wait_ge(filled, 16 * (FILLS - 1))
                all_bodies(pool, run)
                pool.wait_ge(listed[0], 16 * NT * (NG // 2) + 16)
                pool.wait_ge(listed[1], 16 * NT * (NG // 2) + 16)

        def s2(name, shape, dt=F32):
            return sb(name, shape, dt)

        count_i = s2("count_i", [1, 3, NE], I32)
        tiles_of = s2("tiles_of", [1, NE])
        tiles_f = s2("tiles_f", [1, 2, NE])
        past = s2("past", [1, 3, NFT])
        te = s2("te", [1, 3, NFT])
        idx = s2("idx", [128, NFT], I32)
        row_idx = s2("row_idx", [128, 2], I32)
        out_idx = s2("out_idx", [128, 2], I32)
        b2_sb = s2("b2_sb", [128, NE * E])
        got = s2("got", [128, 2, ROW])
        xn = s2("xn", [128, 2, E])
        hb = s2("hb", [128, 4, E])
        xnT = s2("xnT", [KC + 1, 2, 2, FT])
        act_h = s2("act_h", [128, 2, HID])
        hT = s2("hT", [128, PJ, FT])
        y = s2("y", [128, 2, E])
        h_bank = [whole.enter_context(nc.psum_tensor(f"h_bank{n}", [128, 2, 512], F32)) for n in range(2)]
        x_bank = whole.enter_context(nc.psum_tensor("x_bank", [128, 512], F32))
        t_bank = [whole.enter_context(nc.psum_tensor(f"t_bank{n}", [128, 512], F32)) for n in range(2)]
        y_bank = whole.enter_context(nc.psum_tensor("y_bank", [128, 512], F32))

        table_step = sem("table_step")
        table_made = sem("table_made")
        ones_set = sem("ones_set")
        b2_loaded = sem("b2_loaded")
        idx_in = [sem(f"idx_in{n}") for n in range(4)]
        row_idx_made = sem("row_idx_made")
        out_idx_made = sem("out_idx_made")
        gathered = [sem(f"gathered{p}") for p in range(2)]
        xn_made = sem("xn_made")
        hb_made = sem("hb_made")
        xT_written = sem("xT_written")
        xT_read = sem("xT_read")
        h_written = sem("h_written")
        gelu_made = sem("gelu_made")
        hT_written = sem("hT_written")
        hT_read = sem("hT_read")
        y_written = sem("y_written")
        y_made = sem("y_made")
        scattered = [sem(f"scattered{p}") for p in range(2)]

        def all_tiles(eng, run):
            for t in (0, 1):
                run(t, t, 0)
            with eng.Fori(0, (NFT - 6) // 4) as m:
                for j in range(2, 6):
                    run(m * 4 + j, j % 4, m + j // 4)
            for t in range(NFT - 4, NFT):
                run(t, t % 4, t // 4)

        def has_next(t, ahead=1):
            return not (isinstance(t, int) and t + ahead >= NFT)

        def has_former(t):
            return not (isinstance(t, int) and t == 0)

        def column(a, t):
            return a[:, t:t + 1] if isinstance(t, int) else a[:, bass.ds(t, 1)]

        def at(table, t):
            return table[0:1, t:t + 1] if isinstance(t, int) else table[0:1, bass.ds(t, 1)]

        block = whole.enter_context(nc.Block())

        @block.sync
        def _(sp):
            sp.dma_start(b2_sb[:], b2).then_inc(b2_loaded, 16)
            sp.wait_ge(table_made, 1)

            def run(t, slot, q):
                if not (isinstance(t, int) and t < 4):
                    sp.wait_ge(idx_in[slot], q * 16)
                place = sp.value_load(at(tile_place, t), min_val=0, max_val=LIST - FT)
                sp.dma_start(column(idx, t), list_d[bass.ds(place, FT), :]).then_inc(idx_in[slot], 16)

            for t in range(4):
                run(t, t, 0)
            with sp.Fori(1, NFT // 4) as m:
                for j in range(4):
                    run(m * 4 + j, j, m)
            for t in range(NFT - NFT % 4, NFT):
                run(t, t % 4, t // 4)

        @block.gpsimd
        def _(pool):
            def gather(t, slot, q):
                par, k = slot % 2, q * 2 + slot // 2
                pool.wait_ge(idx_in[slot], q * 16 + 16)
                if not (isinstance(t, int) and t < 2):
                    pool.wait_ge(gathered[par], k * 16)
                settle(pool)
                pool.tensor_copy(row_idx[:, par:par + 1], column(idx, t)).then_inc(row_idx_made, 1)
                pool.wait_ge(row_idx_made, t + 1)
                if not (isinstance(t, int) and t < 2):
                    pool.wait_ge(hb_made, t - 1)
                settle(pool)
                pool.indirect_dma_start(out=got[:, par, :], out_offset=None, in_=rows_d,
                                        in_offset=bass.IndirectOffsetOnAxis(
                                            ap=row_idx[:, par:par + 1].bitcast(U32), axis=0),
                                        bounds_check=NTOK, oob_is_err=False).then_inc(gathered[par], 16)

            def scatter(t, slot, k):
                par = slot % 2
                if not (isinstance(t, int) and t < 2):
                    pool.wait_ge(scattered[par], k * 16)
                settle(pool)
                pool.tensor_copy(out_idx[:, par:par + 1], column(idx, t)).then_inc(out_idx_made, 1)
                pool.wait_ge(out_idx_made, t + 1)
                pool.wait_ge(y_made, t + 1)
                settle(pool)
                pool.indirect_dma_start(out=out,
                                        out_offset=bass.IndirectOffsetOnAxis(
                                            ap=out_idx[:, par:par + 1].bitcast(U32), axis=0),
                                        in_=y[:, par, :], in_offset=None, bounds_check=NTOK - 1,
                                        oob_is_err=False).then_inc(scattered[par], 16)

            for t in range(3):
                gather(t, t, 0)

            def run(t, slot, q):
                if has_next(t, 3):
                    gather(t + 3, (slot + 3) % 4, q + (slot + 3) // 4)
                if has_former(t):
                    scatter(t - 1, (slot - 1) % 4, q * 2 + slot // 2 - 1 + slot % 2)

            all_tiles(pool, run)
            scatter(NFT - 1, (NFT - 1) % 4, (NFT - 1) // 2)
            pool.wait_ge(scattered[0], 16 * (NFT // 2))
            pool.wait_ge(scattered[1], 16 * (NFT // 2))

        @block.tensor
        def _(pe):
            pe.wait_ge(table_made, 1)
            pe.wait_ge(ones_set, 1)

            def expert(t):
                return pe.value_load(at(tile_expert, t), min_val=0, max_val=NE - 1)

            def tr_x(t, par):
                pe.wait_ge(xn_made, t + 1)
                wait(pe, xT_read, t)
                for c in range(2):
                    mm = pe.transpose(x_bank[0:KC, c * FT:(c + 1) * FT], xn[:, par, c * KC:(c + 1) * KC],
                                      ident[:, :])
                mm.then_inc(xT_written, 1)

            def up(t, par, e):
                pe.wait_ge(xT_read, t + 1)
                wait(pe, gelu_made, t - 1)
                for f in range(2):
                    for c in range(2):
                        rows = KC + c
                        mm = pe.matmul(h_bank[par][:, f, 0:HID // 2], xnT[0:rows, par, c, :],
                                       w1_sb[0:rows, bass.ds(e, 1), c, f * (HID // 2):(f + 1) * (HID // 2)]
                                       .rearrange("p e n -> p (e n)"), start=(c == 0), stop=(c == 1))
                mm.then_inc(h_written, 1)

            def tr_h(t, par):
                pe.wait_ge(gelu_made, t + 1)
                for b in range(2):
                    wait(pe, hT_read, 2 * t + b - 1)
                    for j in range(3):
                        a = (3 * b + j) * 128
                        mm = pe.transpose(t_bank[b][:, j * FT:(j + 1) * FT], act_h[:, par, a:a + 128], ident[:, :])
                    mm.then_inc(hT_written, 1)

            def down(t, e):
                wait(pe, y_made, t)
                for j in range(PJ):
                    if j % 3 == 0:
                        pe.wait_ge(hT_read, 2 * t + 1 + j // 3)
                    mm = pe.matmul(y_bank[:, 0:E], hT[:, j, :],
                                   w2_sb[:, bass.ds(e, 1), j, :].rearrange("p e n -> p (e n)"),
                                   start=(j == 0), stop=(j == PJ - 1))
                mm.then_inc(y_written, 1)

            tr_x(0, 0)

            def run(t, slot, q):
                par = slot % 2
                e = expert(t)
                if has_former(t):
                    former = expert(t - 1)
                    tr_h(t - 1, 1 - par)
                up(t, par, e)
                if has_next(t):
                    tr_x(t + 1, 1 - par)
                if has_former(t):
                    down(t - 1, former)

            all_tiles(pe, run)
            tr_h(NFT - 1, (NFT - 1) % 2)
            down(NFT - 1, expert(NFT - 1))

        @block.scalar
        def _(act):
            act.wait_ge(ones_set, 1)

            def read_x(t, par):
                act.wait_ge(xT_written, t + 1)
                wait(act, h_written, t - 1)
                act.activation(xnT[0:KC, par, :, :], x_bank[0:KC, 0:2 * FT].rearrange("p (c t) -> p c t", c=2),
                               ACT.Copy).then_inc(xT_read, 1)

            def run(t, slot, q):
                par = slot % 2
                act.wait_ge(h_written, t + 1)
                wait(act, hT_written, 2 * t - 2)
                act.activation(act_h[:, par, :].rearrange("p (f n) -> p f n", f=2),
                               h_bank[par][:, :, 0:HID // 2], ACT.Gelu).then_inc(gelu_made, 1)
                if has_next(t):
                    read_x(t + 1, 1 - par)

            read_x(0, 0)
            all_tiles(act, run)

        @block.vector
        def _(dve):
            n = [0]

            def step(ins):
                n[0] += 1
                ins.then_inc(table_step, 1)
                dve.wait_ge(table_step, n[0])

            step(dve.tensor_tensor(tiles_f[:, 0, :], places[0:1, :], base_sb[0:1, :], ALU.subtract))
            step(dve.tensor_scalar(count_i[:, 0, :], tiles_f[:, 0, :], float(FT - 1), None, ALU.add))
            step(dve.tensor_scalar(count_i[:, 1, :], count_i[:, 0, :], 7, None, ALU.arith_shift_right))
            step(dve.tensor_copy(tiles_of[:, :], count_i[:, 1, :]))
            step(dve.tensor_copy(tiles_f[:, 1, 0:1], tiles_of[:, 0:1]))
            for e in range(1, 3):
                step(dve.tensor_tensor(tiles_f[:, 1, e:e + 1], tiles_f[:, 1, e - 1:e], tiles_of[:, e:e + 1], ALU.add))
            for e in range(3):
                step(dve.tensor_scalar(past[:, e, :], tvec[:, :], tiles_f[:, 1, e:e + 1], None, ALU.is_ge))
            step(dve.tensor_tensor(te[:, 0, :], past[:, 0, :], past[:, 1, :], ALU.add))
            step(dve.tensor_tensor(te[:, 0, :], te[:, 0, :], past[:, 2, :], ALU.add))
            step(dve.tensor_copy(tile_expert[:, :], te[:, 0, :]))
            for e in range(3):
                step(dve.tensor_scalar(past[:, e, :], past[:, e, :], tiles_of[:, e:e + 1], None, ALU.mult))
            step(dve.tensor_tensor(te[:, 1, :], past[:, 0, :], past[:, 1, :], ALU.add))
            step(dve.tensor_tensor(te[:, 1, :], te[:, 1, :], past[:, 2, :], ALU.add))
            step(dve.tensor_tensor(te[:, 2, :], tvec[:, :], te[:, 1, :], ALU.subtract))
            step(dve.tensor_scalar(te[:, 2, :], te[:, 2, :], float(FT), None, ALU.mult))
            step(dve.tensor_scalar(te[:, 0, :], te[:, 0, :], float(CAP), None, ALU.mult))
            step(dve.tensor_tensor(te[:, 2, :], te[:, 2, :], te[:, 0, :], ALU.add))
            dve.tensor_copy(tile_place[:, :], te[:, 2, :]).then_inc(table_made, 1)
            dve.wait_ge(table_made, 1)
            dve.memset(xnT[KC:KC + 1, :, :, :], 1.0).then_inc(ones_set, 1)

            def read_row(t, slot, k, e):
                par = slot % 2
                dve.wait_ge(gathered[par], (k + 1) * 16)
                wait(dve, xT_written, t - 1)
                dve.tensor_scalar(xn[:, par, :], got[:, par, 0:E], got[:, par, E:E + 1], got[:, par, E + 1:E + 2],
                                  ALU.subtract, ALU.mult).then_inc(xn_made, 1)
                wait(dve, y_made, t - 3)
                dve.tensor_tensor(hb[:, slot, :], got[:, par, 0:E], b2_sb[:, bass.ds(e * E, E)],
                                  ALU.add).then_inc(hb_made, 1)

            def read_h(t):
                for b in range(2):
                    dve.wait_ge(hT_written, 2 * t + b + 1)
                    wait(dve, y_written, t)
                    dve.tensor_copy(hT[:, 3 * b:3 * b + 3, :],
                                    t_bank[b][:, 0:3 * FT].rearrange("p (j t) -> p j t", j=3)).then_inc(hT_read, 1)

            def finish(t, slot, k):
                dve.wait_ge(y_written, t + 1)
                dve.wait_ge(hb_made, t + 1)
                if not (isinstance(t, int) and t < 2):
                    dve.wait_ge(scattered[slot % 2], k * 16)
                dve.tensor_tensor(y[:, slot % 2, :], y_bank[:, 0:E], hb[:, slot, :], ALU.add).then_inc(y_made, 1)

            def expert(t):
                return dve.value_load(at(tile_expert, t), min_val=0, max_val=NE - 1)

            dve.wait_ge(b2_loaded, 16)
            for t in range(2):
                read_row(t, t, 0, expert(t))

            def run(t, slot, q):
                k = q * 2 + slot // 2
                if has_next(t, 2):
                    e = expert(t + 2)
                if has_former(t):
                    read_h(t - 1)
                if has_next(t, 2):
                    read_row(t + 2, (slot + 2) % 4, k + 1, e)
                if has_former(t):
                    finish(t - 1, (slot - 1) % 4, k - 1 + slot % 2)

            all_tiles(dve, run)
            read_h(NFT - 1)
            finish(NFT - 1, (NFT - 1) % 4, (NFT - 1) // 2)


N_CONSTS = 21


def kernel(x, L0_tok_W, L0_tok_b, L0_attn_wq, L0_attn_bq, L0_attn_wk, L0_attn_bk, L0_attn_wv, L0_attn_bv,
           L0_attn_wo, L0_attn_bo, L0_ffn_Wg, L0_ffn_bg, L0_ffn_W1, L0_ffn_b1, L0_ffn_W2, L0_ffn_b2):
    import concourse.bacc as bacc
    from concourse.bass_utils import run_bass_kernel_spmd

    def rows(a, n):
        return np.broadcast_to(np.asarray(a)[None], (n,) + np.shape(a))

    def chunks(w, k):
        w = np.asarray(w)
        return w.reshape(k, w.shape[0] // k, w.shape[1]).transpose(1, 0, 2)

    tokens = np.asarray(x).reshape(B, CH, SIDE, PATCH, SIDE, PATCH).transpose(0, 2, 4, 1, 3, 5).reshape(NTOK, PD)
    pos = np.arange(GT, dtype=np.float32) % TOK
    scale = np.float32(10000.0) ** (np.float32(2.0) * np.arange(4, dtype=np.float32) / np.float32(HD))
    angle = (pos[:, None] / scale[None]).astype(np.float32)
    cos, sin = np.cos(angle).astype(np.float32), np.sin(angle).astype(np.float32)
    tables = [np.stack([cos, cos], 1), np.stack([sin, -sin], 1)]
    tables = [a.reshape(NT, TP, 2, 4).transpose(1, 0, 2, 3) for a in tables]
    mask = np.ones((NE, NT), np.float32)
    mask[:, 0] = 0.0
    base = np.arange(NE, dtype=np.float32) * CAP - 1
    arrays = dict(
        xT=tokens.reshape(NTOK // TP, TP, PJ, 128).transpose(0, 3, 2, 1).reshape(NTOK // TP, 128, PJ * TP),
        wtok=chunks(np.asarray(L0_tok_W).T, PJ),
        wqk=chunks(np.concatenate([np.asarray(L0_attn_wq).T, np.asarray(L0_attn_wk).T], 1), 2),
        wv=chunks(np.asarray(L0_attn_wv).T, 2),
        wo=chunks(np.asarray(L0_attn_wo).T, 2),
        w1=np.asarray(L0_ffn_W1).reshape(NE, 2, KC, HID).transpose(2, 0, 1, 3),
        b1=np.asarray(L0_ffn_b1).reshape(1, NE, HID),
        w2=np.asarray(L0_ffn_W2).reshape(NE, PJ, 128, E).transpose(2, 0, 1, 3),
        btok=rows(L0_tok_b, TP),
        bqk=rows(np.concatenate([np.asarray(L0_attn_bq), np.asarray(L0_attn_bk)]), TP),
        bv=rows(L0_attn_bv, QC),
        bo=rows(L0_attn_bo, TP),
        wg=rows(np.asarray(L0_ffn_Wg).T, TP),
        bg=rows(L0_ffn_bg, TP),
        b2=rows(np.asarray(L0_ffn_b2).reshape(NE * E), 128),
        rope_cos=tables[0], rope_sin=tables[1],
        ident_in=np.eye(128, dtype=np.float32),
        tri_in=np.triu(np.ones((TP, TP), np.float32), 1),
        ones_in=np.ones((TP, TP), np.float32),
        scan_mask=rows(mask.reshape(-1), TP),
        desc_in=rows(np.arange(NE, 0, -1, dtype=np.float32), TP),
        base_in=rows(base, TP),
        tokid_in=(np.arange(GT, dtype=np.int32) - GT).reshape(NT, TP).T,
        tvec_in=np.arange(NFT, dtype=np.float32)[None],
    )
    nc = bacc.Bacc("TRN2", target_bir_lowering=False, num_devices=1)
    args, feeds = {}, {}
    for name, a in arrays.items():
        a = np.ascontiguousarray(a)
        feeds[name + "_dram"] = a
        args[name] = nc.dram_tensor(name + "_dram", a.shape, mybir.dt.from_np(a.dtype), kind="ExternalInput").ap()
    args["out"] = nc.dram_tensor("out_dram", (NTOK, E), F32, kind="ExternalOutput").ap()
    build(nc, **args)
    result = run_bass_kernel_spmd(nc, [feeds], core_ids=[0])
    return result.results[0]["out_dram"].reshape(B, TOK, E)
```

```python
from contextlib import ExitStack

import concourse.bass as bass
import numpy as np
from concourse import mybir
from concourse.alu_op_type import AluOpType as ALU

F32 = mybir.dt.float32
BF16 = mybir.dt.bfloat16
I32 = mybir.dt.int32
U32 = mybir.dt.uint32
ACT = mybir.ActivationFunctionType
AX = mybir.AxisListType

B, CH, IMG, PATCH = 64, 3, 224, 16
E, NH, HD = 192, 12, 16
NE, HID = 4, 768
SIDE = IMG // PATCH
TOK = SIDE * SIDE
NTOK = B * TOK
PD = CH * PATCH * PATCH
GI = 4
NG = B // GI
GT = GI * TOK
TP = 112
NT = GT // TP
QC = TOK // 2
KC = E // 2
PJ = PD // 128
HG = KC // HD
HALF = GT // 2
CAP = 98 * 128
FT = 128
NFT = 102
LIST = NE * CAP + 4 * FT
FILLS = 12
ROW = E + 2
EPS = 1e-5
Q_PARTS = [0, 0, 1, 0, 2, 1]
K_PARTS = [0, 1, 0, 2, 0, 1]
NSPLIT = len(Q_PARTS)
SK = NSPLIT * HD
assert NTOK <= CAP and NTOK // FT + NE - 1 <= NFT and LIST % (128 * FILLS) == 0 and SK + 2 <= 128

S_IN_SLOT = [2, 1, 2, 1, 2, 2, 2, 0, 0, 0, 0, 0]
S_HEADS = [list(range(sum(S_IN_SLOT[:s]), sum(S_IN_SLOT[:s + 1]))) for s in range(NH)]
A_TILES = [(0, 1), (2, 3), (4, 5), (6,)]
WO_TILES = [(5, 6), (0,), (1, 2), (3, 4)]
D_TILES = [(3, 4), (5, 6), (0,), (1, 2)]
MAKE = (dict(patchA=0, patchB=0, stats=2, norm=4, trH=5, qk=6, trQ=10),
        dict(patchA=4, patchB=5, stats=5, norm=8, trH=9, qk=11, trQ=15))
V_SLOTS = (6, 8, 11, 11)
FINISH = (("trO", 0, 3), ("trO", 1, 4), ("divide", 0, 3), ("divide", 1, 6), ("trN", 0, 7))
WO_SLOT = 9
ADD_SLOT = 11
D_SLOTS = (10, 11)
ROUTE = ((2, "hot", 3), (2, "route", 7), (2, "place", 8), (3, "list", 10))
MAXIMA = (("negmax", 9), ("trM", 9))


def jobs_of(step, make_next, finish_prev, attend_next):
    image, d, routed = finish_prev
    out = []
    if attend_next:
        out += [(slot, job, 0) for job, slot in MAXIMA]
    if routed:
        out += [(slot, job, 0) for s, job, slot in ROUTE if s == step]
    if make_next:
        for back in (1, 0):
            for slots, t in zip(MAKE, A_TILES[step - back] if step >= back else ()):
                out += [(slot - NH * back, job, t) for job, slot in slots.items() if slot // NH == back]
        if step == 3:
            out += [(slot, "V", m) for m, slot in enumerate(V_SLOTS)]
    if image:
        out += [(slot, job, c) for job, c, slot in FINISH]
        out += [(WO_SLOT, "wo", WO_TILES[step]), (ADD_SLOT, "add", WO_TILES[step])]
    if d:
        out += [(slot, "D", t) for slot, t in zip(D_SLOTS, D_TILES[step])]
    order = sorted(range(len(out)), key=lambda k: (out[k][0], k))
    return [out[k] for k in order]


def prologue_jobs():
    out = []
    for n in range(NT + 3):
        stages = ((("patchA", "patchB", "stats"), n), (("norm", "trH"), n - 1), (("qk",), n - 2), (("trQ",), n - 3))
        out += [(0, job, t) for jobs, t in stages if 0 <= t < NT for job in jobs]
    return out + [(0, "V", m) for m in range(GI)]


def body_jobs(kind):
    if kind == "prologue":
        return [prologue_jobs(), [(0, "negmax", 0), (1, "trM", 0)]]
    if kind == "tail":
        return [jobs_of(0, False, (True, True, False), False), jobs_of(1, False, (False, True, False), False),
                jobs_of(2, False, (False, False, True), False),
                jobs_of(3, False, (False, False, True), False)]
    out = []
    for i in range(GI):
        first, last = kind == "first", kind == "last"
        done = (not (first and i == 0), not (first and i <= 1), not first)
        out.append(jobs_of(i, not last, done, not (last and i == 3)))
    return out


WORK_JOBS = ("patchA", "trH", "qk", "trQ", "V", "trO", "trN", "wo", "trM", "route")
WORK_BANKS = 3
KINDS = ["prologue", "first", "mid", "last", "tail"]


def work_table(kind):
    count, table = [0] * WORK_BANKS, {}
    n = 0
    for i, jobs in enumerate(body_jobs(kind)):
        for _, job, arg in jobs:
            if job in WORK_JOBS:
                b = n % WORK_BANKS
                table[(i, job, arg)] = (b, count[b])
                count[b] += 1
                n += 1
    return table, count


TABLES = {k: work_table(k) for k in KINDS}


def uses_before(kind, g, b):
    c = {k: TABLES[k][1][b] for k in KINDS}
    if kind == "prologue":
        return 0
    if kind == "first":
        return c["prologue"]
    if kind == "mid":
        return (g - 1) * c["mid"] + (c["prologue"] + c["first"])
    n = c["prologue"] + c["first"] + (NG - 2) * c["mid"]
    return n if kind == "last" else n + c["last"]


def wait(eng, sem, value):
    if not (isinstance(value, int) and value <= 0):
        eng.wait_ge(sem, value)


class Body:

    def __init__(self, kind, g, parity, earlier=None, earlier_prev=None):
        self.kind, self.g, self.parity = kind, g, parity
        self.earlier = g // 2 if earlier is None else earlier
        self.earlier_prev = (g - 1) // 2 if earlier is None else earlier_prev
        self.next = g + 1 if kind != "prologue" else 0
        self.next_par = 1 - parity if kind != "prologue" else 0
        self.steps = {"prologue": 0, "tail": 0}.get(kind, GI)

    def bank(self, i, job, arg):
        table = TABLES[self.kind][0]
        b, n = table[(i, job, arg)] if (i, job, arg) in table else table[(i - 1, job, arg)]
        return b, uses_before(self.kind, self.g, b) + n

    def jobs(self, i, slot):
        return [(j, a) for s, j, a in body_jobs(self.kind)[i] if s == slot]

    def finished(self, i, tile_of):
        prev = (tile_of == "wo" and i == 0) or (tile_of == "D" and i <= 1) or tile_of == "route"
        if self.kind == "tail":
            return NG - 1, (NG - 1) % 2, (NG - 1) // 2
        return (self.g - 1, 1 - self.parity, self.earlier_prev) if prev else (self.g, self.parity, self.earlier)


def all_bodies(eng, run):
    run(Body("prologue", 0, 0))
    run(Body("first", 0, 0))
    with eng.Fori(0, (NG - 2) // 2) as pair:
        run(Body("mid", pair * 2 + 1, 1, pair, pair))
        run(Body("mid", pair * 2 + 2, 0, pair + 1, pair))
    run(Body("last", NG - 1, 1))
    run(Body("tail", NG, 0))


def build(nc, xT, wtok, wqk, wv, wo, w1, b1, w2, btok, bqk, bv, bo, wg, bg, b2, rope_cos, rope_sin,
          ident_in, tri_in, ones_in, scan_mask, desc_in, base_in, tokid_in, tvec_in, out):
    rows_d = nc.dram_tensor("token_rows", (NTOK + 1, ROW), F32, kind="Internal").ap()
    parts_d = [nc.dram_tensor(f"parts{f}", (3, 2 * E, HALF), BF16, kind="Internal").ap() for f in range(2)]
    list_d = nc.dram_tensor("expert_lists", (LIST, 1), I32, kind="Internal").ap()

    with ExitStack() as whole:
        def sem(name):
            return whole.enter_context(nc.semaphore(name))

        def sb_in(ctx, name, shape, dt=F32):
            return ctx.enter_context(nc.sbuf_tensor(name, shape, dt))

        def sb(name, shape, dt=F32):
            return sb_in(whole, name, shape, dt)

        w1_sb = sb("w1_sb", [KC + 1, NE, 2, HID])
        w2_sb = sb("w2_sb", [128, NE, PJ, E])
        ident = sb("ident", [128, 128])
        identb = sb("identb", [128, 128], BF16)
        places = sb("places", [TP, NE])
        base_sb = sb("base_sb", [TP, NE])
        tvec = sb("tvec", [1, NFT])
        tile_expert = sb("tile_expert", [1, NFT], I32)
        tile_place = sb("tile_place", [1, NFT], I32)

        wtok_loaded = sem("wtok_loaded")
        loaded = sem("loaded")
        loaded2 = sem("loaded2")
        rows_stored = [sem(f"rows_stored{p}") for p in range(2)]
        filled = sem("filled")
        listed = [sem(f"listed{p}") for p in range(2)]
        consts_set = sem("consts_set")
        pool_set = sem("pool_set")

        waits_passed = sem("waits_passed")

        def settle(eng):
            eng.sem_inc(waits_passed, 1)

        with ExitStack() as ctx:
            def s1(name, shape, dt=F32):
                return sb_in(ctx, name, shape, dt)

            wtok_sb = s1("wtok_sb", [128, PJ, E])
            wqk_sb = s1("wqk_sb", [KC + 1, 2, 2 * E])
            wv_sb = s1("wv_sb", [KC + 1, 2, E])
            wo_sb = s1("wo_sb", [KC + 1, 2, E])
            btok_sb = s1("btok_sb", [TP, E])
            wg_sb = s1("wg_sb", [TP, NE, E])
            bg_sb = s1("bg_sb", [TP, NE])
            cos_sb = s1("cos_sb", [TP, NT, 2, 4])
            sin_sb = s1("sin_sb", [TP, NT, 2, 4])
            tri = s1("tri", [TP, TP])
            ones = s1("ones", [TP, TP])
            mask_sb = s1("mask_sb", [TP, NE * NT])
            desc_sb = s1("desc_sb", [TP, NE])
            tok_now = s1("tok_now", [TP, 2, NT], I32)
            half_neg = s1("half_neg", [TP, 2])
            sentinels = s1("sentinels", [128, LIST // 128 // FILLS], I32)
            nowhere = s1("nowhere", [TP, 1], I32)
            zero_row = s1("zero_row", [1, ROW])

            x_sb = s1("x_sb", [128, NT, PJ, TP])
            h = s1("h", [TP, 2, NT, E])
            stats = s1("stats", [TP, 2, 6])
            mv = s1("mv", [TP, 2, 2])
            rstd = s1("rstd", [TP, 2, 1])
            hn = s1("hn", [TP, 2, E])
            hnT = s1("hnT", [KC + 1, 2, GT])
            qk = s1("qk", [TP, 2, 2 * E])
            rot = s1("rot", [TP, 2 * NH, 2, 4])
            qkT = s1("qkT", [KC, 4, TP])
            parts = [s1(f"part{n}", [KC, 4, GT], BF16) for n in range(3)]
            qst = s1("qst", [SK + 2, NH, GT], BF16)
            kst = s1("kst", [SK + 2, NH, GT], BF16)
            v_sb = s1("v_sb", [QC, 2, 2 * GI, NH, HD + 1])
            nmax = s1("nmax", [QC, 2, NH])
            nrest = s1("nrest", [QC, 2, NH])
            nparts = s1("nparts", [QC, 2, 2 * NH], BF16)
            nT = s1("nT", [2 * NH, TOK], BF16)
            prob = s1("prob", [QC, 4, 2, TOK])
            oT = s1("oT", [128, 3, TOK])
            rden = s1("rden", [QC, 2, NH])
            on = s1("on", [QC, 2, E])
            onT = s1("onT", [KC + 1, 2, GT])
            h2 = s1("h2", [TP, 2, NT, ROW])
            stats2 = s1("stats2", [TP, 2, 6])
            hn2 = s1("hn2", [TP, E])
            junk = s1("junk", [TP, NE, E])
            logit = s1("logit", [TP, NE, NT])
            top = s1("top", [TP, NT])
            pick = s1("pick", [TP, NE, NT])
            hot = s1("hot", [TP, NE, NT])
            seen = s1("seen", [TP, NE, NT])
            start = s1("start", [TP, NE])
            place = s1("place", [TP, NE, NT])
            place1 = s1("place1", [TP, NT])
            place_i = s1("place_i", [TP, 2, NT], I32)

            s_bank = [ctx.enter_context(nc.psum_tensor(f"s_bank{n}", [128, 512], F32)) for n in range(2)]
            st_bank = [ctx.enter_context(nc.psum_tensor(f"st_bank{n}", [128, 512], F32)) for n in range(2)]
            o_bank = ctx.enter_context(nc.psum_tensor("o_bank", [128, 512], F32))
            work = [ctx.enter_context(nc.psum_tensor(f"work{n}", [128, 512], F32)) for n in range(WORK_BANKS)]

            work_written = [sem(f"work_written{n}") for n in range(WORK_BANKS)]
            work_read = [sem(f"work_read{n}") for n in range(WORK_BANKS)]
            x_in = [sem(f"x_in{t}") for t in range(NT)]
            stats_made = sem("stats_made")
            mv_made = sem("mv_made")
            eps_added = sem("eps_added")
            rstd_made = sem("rstd_made")
            hn_made = sem("hn_made")
            rope_step = sem("rope_step")
            roped = sem("roped")
            split_step = sem("split_step")
            split_made = sem("split_made")
            parts_out = [sem(f"parts_out{f}") for f in range(2)]
            stacked = [sem(f"stacked{f}") for f in range(2)]
            s_written = sem("s_written")
            max_made = sem("max_made")
            nmax_step = sem("nmax_step")
            nparts_made = sem("nparts_made")
            shifted = sem("shifted")
            st_written = sem("st_written")
            exp_made = sem("exp_made")
            pv_written = sem("pv_written")
            o_read = sem("o_read")
            rden_made = sem("rden_made")
            h2_made = sem("h2_made")
            stats2_made = sem("stats2_made")
            mv2_made = sem("mv2_made")
            eps2_added = sem("eps2_added")
            rstd2_made = sem("rstd2_made")
            hn2_made = sem("hn2_made")
            logit_made = sem("logit_made")
            route_step = sem("route_step")
            seen_made = sem("seen_made")
            placed = sem("placed")
            o_cleared = sem("o_cleared")

            STACK_INC = 16 * 2 * NSPLIT
            HOT_STEPS, ROUTE_STEPS = 6, 11

            block = ctx.enter_context(nc.Block())

            @block.sync
            def _(sp):
                def load_x(group, t):
                    if isinstance(group, int):
                        src = xT[group * NT + t]
                    else:
                        src = xT.rearrange("(g t) p n -> g t p n", t=NT)[bass.ds(group, 1), t, :, :].rearrange(
                            "g p n -> (g p) n")
                    sp.dma_start(x_sb[:, t, :, :].rearrange("p j n -> p (j n)"), src).then_inc(x_in[t], 16)

                for t in range(2):
                    load_x(0, t)
                sp.dma_start(wtok_sb[:], wtok).then_inc(wtok_loaded, 16)
                consts = [(btok_sb, btok), (ident, ident_in), (wqk_sb[0:KC], wqk), (wqk_sb[KC:KC + 1, 1, :], bqk),
                          (cos_sb, rope_cos), (sin_sb, rope_sin), (wv_sb[0:KC], wv), (wv_sb[KC:KC + 1, 1, :], bv),
                          (wo_sb[0:KC], wo), (wo_sb[KC:KC + 1, 1, :], bo), (wg_sb, wg), (bg_sb, bg), (tri, tri_in), (ones, ones_in),
                          (mask_sb, scan_mask), (desc_sb, desc_in), (base_sb, base_in), (places, base_in),
                          (tok_now[:, 1, :], tokid_in), (tvec, tvec_in)]
                for dst, src in consts:
                    d = dst if isinstance(dst, bass.AP) else dst[tuple([slice(None)] * len(dst.shape))]
                    sp.dma_start(d, src).then_inc(loaded, 16)
                assert len(consts) == N_CONSTS
                for t in range(2, NT):
                    load_x(0, t)

                def prepare_phase2():
                    sp.dma_start(w1_sb[0:KC], w1).then_inc(loaded2, 16)
                    sp.dma_start(w1_sb[KC:KC + 1, :, 1, :], b1).then_inc(loaded2, 16)
                    sp.dma_start(w2_sb[:], w2).then_inc(loaded2, 16)
                    sp.wait_ge(consts_set, 5)
                    for f in range(FILLS):
                        sp.dma_start(list_d.rearrange("(f p n) o -> f p (n o)", f=FILLS, p=128)[f],
                                     sentinels[:]).then_inc(filled if f else rows_stored[0], 16)
                    sp.wait_ge(filled, 16 * (FILLS - 1))
                    sp.dma_start(rows_d[NTOK:NTOK + 1, :], zero_row[:]).then_inc(rows_stored[1], 16)

                def stack(group, f):
                    wait(sp, split_made, group * NT + (4 if f == 0 else 7))
                    settle(sp)
                    wait(sp, st_written, (group * GI + 2 * f - 2) * NH)
                    settle(sp)
                    cols = slice(f * HALF, (f + 1) * HALF)
                    wait(sp, stacked[f], group * STACK_INC)
                    for which in range(3):
                        sp.dma_start(parts_d[f][which].rearrange("(c p) t -> p c t", c=4),
                                     parts[which][:, :, cols]).then_inc(parts_out[f], 16)
                    sp.wait_ge(parts_out[f], (group + 1) * 48)
                    for n in range(NSPLIT):
                        for dst, a, which in ((qst, 0, Q_PARTS[n]), (kst, E, K_PARTS[n])):
                            sp.dma_start(dst[n * HD:(n + 1) * HD, :, cols],
                                         parts_d[f][which, a:a + E].rearrange("(h d) t -> d h t", d=HD)
                                         ).then_inc(stacked[f], 16)

                def shift(i, step):
                    b, n = step
                    sp.wait_ge(work_read[b], n + 1)
                    for s in range(2):
                        sp.dma_start(qst[SK + s:SK + s + 1, :, i * TOK:(i + 1) * TOK],
                                     nT[s * NH:(s + 1) * NH, :]
                                     ).then_inc(shifted, 16)

                def run(bd):
                    g = bd.g
                    if bd.kind == "prologue":
                        for t in range(NT):
                            load_next(bd, 0, t)
                        stack(0, 0)
                        shift(0, bd.bank(1, "trM", 0))
                        prepare_phase2()
                        return
                    if bd.kind == "tail":
                        store_rows(NG - 1, (NG - 1) % 2)
                        return
                    for i in range(GI):
                        if i == 0:
                            stack(g, 1)
                        if i == 2 and bd.kind != "last":
                            stack(g + 1, 0)
                        if i == 2 and bd.kind != "first":
                            store_rows(g - 1, 1 - bd.parity)
                        for t in A_TILES[i]:
                            if bd.kind == "last":
                                break
                            if isinstance(g, int) and g + 2 >= NG:
                                break
                            load_next(bd, i, t)
                        if not (bd.kind == "last" and i == 3):
                            shift((i + 1) % GI, bd.bank(i, "trM", 0))

                def load_next(bd, i, t):
                    b, n = bd.bank(i, "patchA", t)
                    sp.wait_ge(work_read[b], n + 1)
                    load_x(bd.next + 1, t)

                def store_rows(group, par):
                    sp.wait_ge(rstd2_made, group * NT + NT)
                    dst = (rows_d[0:NTOK].rearrange("(g t p) c -> g p t c", t=NT, p=TP)[group]
                           if isinstance(group, int) else
                           rows_d[0:NTOK].rearrange("(g t p) c -> g p t c", t=NT, p=TP)[bass.ds(group, 1)]
                           .rearrange("g p t c -> (g p) t c"))
                    sp.dma_start(dst, h2[:, par, :, :]).then_inc(rows_stored[par], 16)

                run(Body("prologue", 0, 0))
                run(Body("first", 0, 0))
                with sp.Fori(0, (NG - 2) // 2 - 1) as pair:
                    run(Body("mid", pair * 2 + 1, 1, pair, pair))
                    run(Body("mid", pair * 2 + 2, 0, pair + 1, pair))
                run(Body("mid", NG - 3, 1))
                run(Body("mid", NG - 2, 0))
                run(Body("last", NG - 1, 1))
                run(Body("tail", NG, 0))
                sp.wait_ge(rows_stored[0], 16 * (NG // 2 + 1))
                sp.wait_ge(rows_stored[1], 16 * (NG // 2 + 1))
                sp.wait_ge(loaded2, 48)

            @block.tensor
            def _(pe):
                def wait_read(bd, i, job, arg):
                    b, n = bd.bank(i, job, arg)
                    pe.wait_ge(work_read[b], n + 1)

                def begin(bd, i, job, arg):
                    b, n = bd.bank(i, job, arg)
                    wait(pe, work_read[b], n)
                    return work[b], work_written[b]

                def patchA(bd, i, t):
                    bank, written = begin(bd, i, "patchA", t)
                    pe.wait_ge(x_in[t], (bd.next + 1) * 16)
                    for j in range(PJ // 2):
                        pe.matmul(bank[0:TP, 0:E], x_sb[:, t, j, :], wtok_sb[:, j, :], start=(j == 0), stop=False)

                def patchB(bd, i, t):
                    b, _ = bd.bank(i, "patchA", t)
                    bank, written = work[b], work_written[b]
                    for j in range(PJ // 2, PJ):
                        mm = pe.matmul(bank[0:TP, 0:E], x_sb[:, t, j, :], wtok_sb[:, j, :],
                                       start=(j == 0), stop=(j == PJ - 1))
                    mm.then_inc(written, 1)

                def trH(bd, i, t):
                    T = bd.next * NT + t
                    if bd.kind == "prologue" and t == 0:
                        pe.wait_ge(loaded, 16 * N_CONSTS)
                        pe.wait_ge(consts_set, 5)
                        pe.wait_ge(o_cleared, 1)
                    bank, written = begin(bd, i, "trH", t)
                    pe.wait_ge(hn_made, T + 1)
                    tp = (bd.next_par + t) % 2
                    for c in range(2):
                        mm = pe.transpose(bank[0:KC, c * TP:(c + 1) * TP], hn[:, tp, c * KC:(c + 1) * KC],
                                          ident[0:TP, 0:TP])
                    mm.then_inc(written, 1)

                def qk_product(bd, i, t):
                    bank, written = begin(bd, i, "qk", t)
                    wait_read(bd, i, "trH", t)
                    for c in range(2):
                        mm = pe.matmul(bank[0:TP, 0:2 * E], hnT[0:KC + c, c, t * TP:(t + 1) * TP],
                                       wqk_sb[0:KC + c, c, :],
                                       start=(c == 0), stop=(c == 1))
                    mm.then_inc(written, 1)

                def trQ(bd, i, t):
                    T = bd.next * NT + t
                    bank, written = begin(bd, i, "trQ", t)
                    pe.wait_ge(roped, T + 1)
                    tp = (bd.next_par + t) % 2
                    for c in range(4):
                        mm = pe.transpose(bank[0:KC, c * TP:(c + 1) * TP], qk[:, tp, c * KC:(c + 1) * KC],
                                          ident[0:TP, 0:TP])
                    mm.then_inc(written, 1)

                def v_product(bd, i, m):
                    bank, written = begin(bd, i, "V", m)
                    wait_read(bd, i, "trH", NT - 1)
                    for k in range(2):
                        for c in range(2):
                            a = (2 * m + k) * QC
                            mm = pe.matmul(bank[0:QC, k * E:(k + 1) * E], hnT[0:KC + c, c, a:a + QC],
                                           wv_sb[0:KC + c, c, :],
                                           start=(c == 0), stop=(c == 1))
                    mm.then_inc(written, 1)

                def trO(bd, i, c, image):
                    bank, written = begin(bd, i, "trO", c)
                    pe.wait_ge(o_read, (image + 1) * 3)
                    for q in range(3):
                        mm = pe.transpose(bank[0:QC, q * 128:(q + 1) * 128], oT[:, q, c * QC:(c + 1) * QC],
                                          ident[:, :])
                    mm.then_inc(written, 1)

                def trN(bd, i, image):
                    bank, written = begin(bd, i, "trN", 0)
                    wait_read(bd, i, "trO", 1)
                    for c in range(2):
                        for k in range(2):
                            mm = pe.transpose(bank[0:KC, c * TOK + k * QC:c * TOK + (k + 1) * QC],
                                              on[:, k, c * KC:(c + 1) * KC], ident[0:QC, 0:QC])
                    mm.then_inc(written, 1)

                def wo_product(bd, i, tiles, image):
                    bank, written = begin(bd, i, "wo", tiles)
                    wait_read(bd, i, "trN", 0)
                    for n, t in enumerate(tiles):
                        for c in range(2):
                            mm = pe.matmul(bank[0:TP, n * E:(n + 1) * E], onT[0:KC + c, c, t * TP:(t + 1) * TP],
                                           wo_sb[0:KC + c, c, :], start=(c == 0), stop=(c == 1))
                    mm.then_inc(written, 1)

                def trM(bd, i, image):
                    bank, written = begin(bd, i, "trM", 0)
                    pe.wait_ge(nparts_made, image + 1)
                    narrow = bank[:, :].bitcast(BF16)
                    for k in range(2):
                        mm = pe.transpose(narrow[0:2 * NH, k * QC:(k + 1) * QC],
                                          nparts[:, k, :], identb[0:QC, 0:QC])
                    mm.then_inc(written, 1)

                def route(bd, i, group):
                    bank, written = begin(bd, i, "route", 0)
                    pe.wait_ge(seen_made, group + 1)
                    pe.matmul(bank[0:TP, 0:NE], tri[:, :], seen[:, :, NT - 1], start=True, stop=True)
                    pe.matmul(bank[0:TP, NE:2 * NE], ones[:, :], seen[:, :, NT - 1], start=True,
                              stop=True).then_inc(written, 1)

                def scores(image, i, hd):
                    if hd == 0:
                        f = (i % GI) // 2
                        group = image // GI if isinstance(image, int) else image_group(image, i)
                        pe.wait_ge(stacked[f], (group + 1) * STACK_INC)
                    H = image * NH + hd
                    wait(pe, max_made, H - 1)
                    a = (i % GI) * TOK
                    for k in range(2):
                        mm = pe.matmul(s_bank[hd % 2][0:QC, k * TOK:(k + 1) * TOK],
                                       qst[0:SK, hd, a + k * QC:a + (k + 1) * QC], kst[0:SK, hd, a:a + TOK],
                                       start=True, stop=True)
                    mm.then_inc(s_written, 1)

                def image_group(image, i):
                    return groups_at[0] + (1 if i == GI else 0)

                groups_at = [0]

                def scores_T(image, i, hd):
                    if hd == 0:
                        pe.wait_ge(shifted, (image + 1) * 32)
                    H = image * NH + hd
                    wait(pe, exp_made, H - 1)
                    a = i * TOK
                    for k in range(2):
                        mm = pe.matmul(st_bank[hd % 2][0:QC, k * TOK:(k + 1) * TOK],
                                       kst[:, hd, a + k * QC:a + (k + 1) * QC], qst[:, hd, a:a + TOK],
                                       start=True, stop=True)
                    mm.then_inc(st_written, 1)

                def pv(image, i, par, hd):
                    H = image * NH + hd
                    pe.wait_ge(exp_made, H + 1)
                    if hd % 4 == 0:
                        wait(pe, o_read, image * 3 + hd // 4)
                    q = hd % 4
                    for k in range(2):
                        mm = pe.matmul(o_bank[32 * q:32 * q + HD + 1, 0:TOK], v_sb[:, par, 2 * i + k, hd, :],
                                       prob[:, hd % 4, k, :], start=(k == 0), stop=(k == 1),
                                       tile_position=(0, 32 * q))
                    mm.then_inc(pv_written, 1)

                def do_jobs(bd, i, slot, image):
                    for job, arg in bd.jobs(i, slot):
                        if job == "patchA":
                            patchA(bd, i, arg)
                        elif job == "patchB":
                            patchB(bd, i, arg)
                        elif job == "trH":
                            trH(bd, i, arg)
                        elif job == "qk":
                            qk_product(bd, i, arg)
                        elif job == "trQ":
                            trQ(bd, i, arg)
                        elif job == "V":
                            v_product(bd, i, arg)
                        elif job == "trO":
                            trO(bd, i, arg, image - 1)
                        elif job == "trN":
                            trN(bd, i, image - 1)
                        elif job == "wo":
                            wo_product(bd, i, arg, image - 1)
                        elif job == "trM":
                            trM(bd, i, image + 1)
                        elif job == "route":
                            route(bd, i, bd.finished(i, "route")[0])

                def run(bd):
                    groups_at[0] = bd.g
                    if bd.kind == "prologue":
                        do_jobs(bd, 0, 0, 0)
                        for hd in range(NH):
                            scores(0, 0, hd)
                        do_jobs(bd, 1, 1, -1)
                        return
                    if bd.kind == "tail":
                        for hd in (NH - 2, NH - 1):
                            pv(B - 1, GI - 1, (NG - 1) % 2, hd)
                        for i in range(len(body_jobs(bd.kind))):
                            for slot in range(NH):
                                do_jobs(bd, i, slot, B)
                        return
                    for i in range(GI):
                        image = bd.g * GI + i
                        for slot in range(NH):
                            if not (bd.kind == "last" and i == GI - 1):
                                for hd in S_HEADS[slot]:
                                    scores(image + 1, i + 1, hd)
                            scores_T(image, i, slot)
                            do_jobs(bd, i, slot, image)
                            if slot >= 2:
                                pv(image, i, bd.parity, slot - 2)
                            elif not (bd.kind == "first" and i == 0):
                                pv(image - 1, (i - 1) % GI, bd.parity if i else 1 - bd.parity, NH - 2 + slot)

                pe.wait_ge(wtok_loaded, 16)
                all_bodies(pe, run)

            @block.scalar
            def _(act):
                def copy(out_, in_):
                    return act.activation(out_, in_, ACT.Copy)

                def do_jobs(bd, i, slot, image):
                    for job, arg in bd.jobs(i, slot):
                        if job not in ("trH", "qk", "trQ", "V", "trN", "trM"):
                            continue
                        b, n = bd.bank(i, job, arg)
                        act.wait_ge(work_written[b], n + 1)
                        bank, read = work[b], work_read[b]
                        if job == "trH":
                            ins = copy(hnT[0:KC, :, arg * TP:(arg + 1) * TP],
                                       bank[0:KC, 0:2 * TP].rearrange("p (c t) -> p c t", c=2))
                            ins.then_inc(read, 1)
                        elif job == "qk":
                            wait(act, split_made, bd.next * NT + arg - 1)
                            copy(qk[:, (bd.next_par + arg) % 2, :], bank[0:TP, 0:2 * E]).then_inc(read, 1)
                        elif job == "V":
                            wait(act, pv_written, (bd.next - 1) * GI * NH)
                            copy(v_sb[:, bd.next_par, 2 * arg:2 * arg + 2, :, 0:HD],
                                 bank[0:QC, 0:2 * E].rearrange("p (k h d) -> p k h d", k=2, d=HD)).then_inc(read, 1)
                        elif job == "trQ":
                            T = bd.next * NT + arg
                            wait(act, split_made, T)
                            wait(act, parts_out[0 if arg < 3 else 1], bd.next * 48)
                            if arg == 3:
                                wait(act, parts_out[0], bd.next * 48)
                            view = bank[0:KC, 0:4 * TP].rearrange("p (c t) -> p c t", c=4)
                            copy(qkT[:, :, :], view)
                            copy(parts[0][:, :, arg * TP:(arg + 1) * TP], view).then_inc(read, 1)
                        elif job == "trN":
                            a = ((i - 1) % GI) * TOK
                            copy(onT[0:KC, :, a:a + TOK],
                                 bank[0:KC, 0:2 * TOK].rearrange("p (c t) -> p c t", c=2)).then_inc(read, 1)
                        else:
                            wait(act, shifted, (image + 1) * 32)
                            copy(nT[:, :], bank[:, :].bitcast(BF16)[0:2 * NH, 0:TOK]).then_inc(read, 1)

                def read_o(image, q, before=None):
                    act.wait_ge(pv_written, image * NH + 4 * q + 4)
                    if before is not None:
                        b, n = before
                        act.wait_ge(work_written[b], n + 1)
                    copy(oT[:, q, :], o_bank[:, 0:TOK]).then_inc(o_read, 1)

                def run(bd):
                    if bd.kind == "prologue":
                        do_jobs(bd, 0, 0, 0)
                        do_jobs(bd, 1, 1, -1)
                        return
                    if bd.kind == "tail":
                        read_o(B - 1, 2)
                        for i in range(len(body_jobs(bd.kind))):
                            for slot in range(NH):
                                do_jobs(bd, i, slot, B)
                        return
                    for i in range(GI):
                        image = bd.g * GI + i
                        start_up = bd.kind == "first" and i == 0
                        for slot in range(NH):
                            if slot == 2 and not start_up:
                                read_o(image - 1, 2)
                            if slot == 6:
                                read_o(image, 0, None if start_up else bd.bank(i, "trO", 1))
                            if slot == 10:
                                read_o(image, 1)
                            H = image * NH + slot
                            act.wait_ge(st_written, H + 1)
                            wait(act, pv_written, H - 3)
                            act.activation(prob[:, slot % 4, :, :],
                                           st_bank[slot % 2][0:QC, 0:2 * TOK].rearrange("p (k t) -> p k t", k=2),
                                           ACT.Exp, scale=float(HD) ** -0.5).then_inc(exp_made, 1)
                            do_jobs(bd, i, slot, image)

                all_bodies(act, run)

            @block.vector
            def _(dve):
                def chain(ins, s, value):
                    ins.then_inc(s, 1)
                    dve.wait_ge(s, value)

                def reader(bd, i, job, arg):
                    b, n = bd.bank(i, job, arg)
                    dve.wait_ge(work_written[b], n + 1)
                    return work[b], work_read[b], n

                def patch(bd, i, t):
                    T = bd.next * NT + t
                    par, tp = bd.next_par, (bd.next_par + t) % 2
                    bank, read, n = reader(bd, i, "patchA", t)
                    dve.tensor_tensor(h[:, par, t, :], bank[0:TP, 0:E], btok_sb[:, :], ALU.add).then_inc(read, 1)
                    dve.wait_ge(read, n + 1)
                    chain(dve.bn_stats(stats[:, tp, :], h[:, par, t, :]), stats_made, T + 1)
                    settle(dve)
                    dve.bn_aggr(mv[:, tp, :], stats[:, tp, :]).then_inc(mv_made, 1)

                def norm(bd, t):
                    T = bd.next * NT + t
                    par, tp = bd.next_par, (bd.next_par + t) % 2
                    dve.wait_ge(rstd_made, T + 1)
                    dve.tensor_scalar(hn[:, tp, :], h[:, par, t, :], mv[:, tp, 0:1], rstd[:, tp, 0:1],
                                      ALU.subtract, ALU.mult).then_inc(hn_made, 1)

                def divide(bd, i, c, image):
                    bank, read, n = reader(bd, i, "trO", c)
                    view = bank[0:QC, 0:3 * 128].rearrange("p (h d) -> p h d", d=32)
                    chain(dve.reciprocal(rden[:, c, :], view[:, :, HD]), rden_made, 2 * image + c + 1)
                    dve.tensor_tensor(on[:, c, :].rearrange("p (h d) -> p h d", d=HD), view[:, :, 0:HD],
                                      rden[:, c, :].unsqueeze(2).to_broadcast([QC, NH, HD]),
                                      ALU.mult).then_inc(read, 1)

                def residual(bd, i, tiles):
                    group, par, earlier = bd.finished(i, "wo")
                    bank, read, n = reader(bd, i, "wo", tiles)
                    dve.wait_ge(rows_stored[par], 16 * (earlier + 1))
                    m = len(tiles)
                    dve.tensor_tensor(h2[:, par, tiles[0]:tiles[0] + m, 0:E],
                                      bank[0:TP, 0:m * E].rearrange("p (t c) -> p t c", t=m),
                                      h[:, par, tiles[0]:tiles[0] + m, :], ALU.add).then_inc(read, 1)
                    dve.wait_ge(read, n + 1)
                    for t in tiles:
                        T = group * NT + t
                        chain(dve.bn_stats(stats2[:, t % 2, :], h2[:, par, t, 0:E]), stats2_made, T + 1)
                        settle(dve)
                        dve.bn_aggr(h2[:, par, t, E:E + 2], stats2[:, t % 2, :]).then_inc(mv2_made, 1)

                def logits(bd, i, t):
                    group, par, _ = bd.finished(i, "D")
                    T = group * NT + t
                    dve.wait_ge(rstd2_made, T + 1)
                    wait(dve, logit_made, T)
                    chain(dve.tensor_scalar(hn2[:, :], h2[:, par, t, 0:E], h2[:, par, t, E:E + 1],
                                            h2[:, par, t, E + 1:E + 2], ALU.subtract, ALU.mult), hn2_made, T + 1)
                    for e in range(NE):
                        ins = dve.tensor_tensor_reduce(junk[:, e, :], hn2[:, :], wg_sb[:, e, :], 1.0, 0.0, ALU.mult,
                                                       ALU.add, logit[:, e, t:t + 1])
                    ins.then_inc(logit_made, 1)

                def over_tiles(a):
                    return a.unsqueeze(2).to_broadcast([TP, NE, NT])

                def over_experts(a):
                    return a.unsqueeze(1).to_broadcast([TP, NE, NT])

                def hot_experts(bd, i):
                    group, _, _ = bd.finished(i, "route")
                    n = [0]

                    def step(ins):
                        n[0] += 1
                        chain(ins, route_step, group * ROUTE_STEPS + n[0])

                    dve.wait_ge(logit_made, group * NT + NT)
                    step(dve.tensor_tensor(logit[:, :, :], logit[:, :, :], over_tiles(bg_sb[:, :]), ALU.add))
                    step(dve.tensor_reduce(top[:, :], logit[:, :, :].rearrange("p e t -> p t e"), AX.X, ALU.max))
                    step(dve.tensor_tensor(pick[:, :, :], logit[:, :, :], over_experts(top[:, :]), ALU.is_ge))
                    step(dve.tensor_tensor(pick[:, :, :], pick[:, :, :], over_tiles(desc_sb[:, :]), ALU.mult))
                    step(dve.tensor_reduce(top[:, :], pick[:, :, :].rearrange("p e t -> p t e"), AX.X, ALU.max))
                    step(dve.tensor_tensor(hot[:, :, :], pick[:, :, :], over_experts(top[:, :]), ALU.is_equal))
                    dve.tensor_tensor_scan(seen[:, :, :].rearrange("p e t -> p (e t)"), mask_sb[:, :],
                                           hot[:, :, :].rearrange("p e t -> p (e t)"), 0.0, ALU.mult,
                                           ALU.add).then_inc(seen_made, 1)
                    assert n[0] == HOT_STEPS

                def places_of(bd, i):
                    group, par, earlier = bd.finished(i, "route")
                    n = [HOT_STEPS]

                    def step(ins):
                        n[0] += 1
                        chain(ins, route_step, group * ROUTE_STEPS + n[0])

                    bank, read, m = reader(bd, i, "route", 0)
                    step(dve.tensor_tensor(start[:, :], bank[0:TP, 0:NE], places[:, :], ALU.add))
                    dve.tensor_tensor(places[:, :], bank[0:TP, NE:2 * NE], places[:, :], ALU.add).then_inc(read, 1)
                    dve.wait_ge(read, m + 1)
                    step(dve.tensor_tensor(place[:, :, :], seen[:, :, :], over_tiles(start[:, :]), ALU.add))
                    step(dve.tensor_tensor(place[:, :, :], place[:, :, :], hot[:, :, :], ALU.mult))
                    step(dve.tensor_reduce(place1[:, :], place[:, :, :].rearrange("p e t -> p t e"), AX.X, ALU.add))
                    dve.wait_ge(listed[par], earlier * (16 * NT) + 16)
                    step(dve.tensor_scalar(tok_now[:, par, :], tok_now[:, 1 - par, :], float(GT), None, ALU.add))
                    dve.tensor_copy(place_i[:, par, :], place1[:, :]).then_inc(placed, 1)
                    assert n[0] == ROUTE_STEPS

                def row_max(image, hd):
                    H = image * NH + hd
                    dve.wait_ge(s_written, H + 1)
                    if hd == 0:
                        wait(dve, nparts_made, image)
                    dve.tensor_reduce(nmax[:, :, hd], s_bank[hd % 2][0:QC, 0:2 * TOK].rearrange(
                        "p (k t) -> p k t", k=2), AX.X, ALU.max, negate=True).then_inc(max_made, 1)

                def split_max(image):
                    dve.wait_ge(max_made, (image + 1) * NH)
                    wait(dve, shifted, image * 32)
                    chain(dve.tensor_copy(nparts[:, :, 0:NH], nmax[:, :, :]), nmax_step, 2 * image + 1)
                    chain(dve.tensor_tensor(nrest[:, :, :], nmax[:, :, :], nparts[:, :, 0:NH], ALU.subtract),
                          nmax_step, 2 * image + 2)
                    dve.tensor_copy(nparts[:, :, NH:2 * NH], nrest[:, :, :]).then_inc(nparts_made, 1)

                def do_jobs(bd, i, slot, image):
                    for job, arg in bd.jobs(i, slot):
                        if job == "stats":
                            patch(bd, i, arg)
                        elif job == "norm":
                            norm(bd, arg)
                        elif job == "divide":
                            divide(bd, i, arg, image - 1)
                        elif job == "add":
                            residual(bd, i, arg)
                        elif job == "D":
                            logits(bd, i, arg)
                        elif job == "hot":
                            hot_experts(bd, i)
                        elif job == "place":
                            places_of(bd, i)
                        elif job == "negmax":
                            split_max(image + 1)

                def run(bd):
                    if bd.kind == "prologue":
                        do_jobs(bd, 0, 0, 0)
                        for hd in range(NH):
                            row_max(0, hd)
                        do_jobs(bd, 1, 0, -1)
                        return
                    if bd.kind == "tail":
                        for i in range(len(body_jobs(bd.kind))):
                            for slot in range(NH):
                                do_jobs(bd, i, slot, B)
                        return
                    for i in range(GI):
                        image = bd.g * GI + i
                        for slot in range(NH):
                            if not (bd.kind == "last" and i == GI - 1):
                                for hd in S_HEADS[slot]:
                                    row_max(image + 1, hd)
                            do_jobs(bd, i, slot, image)

                dve.memset(o_bank[:, :], 0.0).then_inc(o_cleared, 1)
                dve.memset(hnT[KC:KC + 1, :, :], 1.0).then_inc(consts_set, 1)
                dve.memset(onT[KC:KC + 1, :, :], 1.0).then_inc(consts_set, 1)
                dve.memset(v_sb[:, :, :, :, HD:HD + 1].rearrange("p a b h o -> p (a b h) o"), 1.0).then_inc(consts_set, 1)
                dve.wait_ge(loaded, 16 * N_CONSTS)
                dve.tensor_copy(identb[:, :], ident[:, :]).then_inc(consts_set, 1)
                all_bodies(dve, run)

            @block.gpsimd
            def _(pool):
                def power(dst, variance, s_eps, s_done, T, n):
                    settle(pool)
                    pool.tensor_scalar(dst, variance, EPS, None, ALU.add).then_inc(s_eps, n)
                    pool.wait_ge(s_eps, T + 1)
                    pool.tensor_tensor(dst, dst, half_neg[:, 0:n], ALU.pow).then_inc(s_done, n)

                def patch(bd, t):
                    T = bd.next * NT + t
                    tp = (bd.next_par + t) % 2
                    pool.wait_ge(mv_made, T + 1)
                    wait(pool, hn_made, T - 1)
                    power(rstd[:, tp, :], mv[:, tp, 1:2], eps_added, rstd_made, T, 1)

                def rope(bd, i, t):
                    T = bd.next * NT + t
                    b, n = bd.bank(i, "qk", t)
                    pool.wait_ge(work_read[b], n + 1)
                    view = qk[:, (bd.next_par + t) % 2, :].rearrange("p (h a d) -> p h a d", a=2, d=HD // 2)
                    first = view[:, :, :, 0:4]

                    def table(x):
                        return x[:, t, :, :].unsqueeze(1).to_broadcast([TP, 2 * NH, 2, 4])

                    wait(pool, roped, T)
                    pool.tensor_tensor(rot[:, :, :, :], first, table(sin_sb), ALU.mult).then_inc(rope_step, 1)
                    pool.wait_ge(rope_step, 3 * T + 1)
                    pool.tensor_tensor(first, first, table(cos_sb), ALU.mult).then_inc(rope_step, 1)
                    pool.wait_ge(rope_step, 3 * T + 2)
                    pool.tensor_tensor(first[:, :, 0, :], first[:, :, 0, :], rot[:, :, 1, :],
                                       ALU.add).then_inc(rope_step, 1)
                    pool.wait_ge(rope_step, 3 * T + 3)
                    pool.tensor_tensor(first[:, :, 1, :], first[:, :, 1, :], rot[:, :, 0, :],
                                       ALU.add).then_inc(roped, 1)

                def split(bd, i, t):
                    T = bd.next * NT + t
                    cols = slice(t * TP, (t + 1) * TP)
                    b, n = bd.bank(i, "trQ", t)
                    pool.wait_ge(work_read[b], n + 1)
                    pool.tensor_tensor(parts[1][:, :, cols], qkT[:, :, :], parts[0][:, :, cols], ALU.subtract)
                    pool.tensor_tensor(qkT[:, :, :], qkT[:, :, :], parts[0][:, :, cols],
                                       ALU.subtract).then_inc(split_step, 1)
                    pool.wait_ge(split_step, T + 1)
                    pool.tensor_tensor(parts[2][:, :, cols], qkT[:, :, :], parts[1][:, :, cols],
                                       ALU.subtract).then_inc(split_made, 1)

                def statistics2(bd, i, tiles):
                    group, par, _ = bd.finished(i, "wo")
                    T = group * NT + tiles[-1]
                    var = h2[:, par, tiles[0]:tiles[-1] + 1, E + 1]
                    pool.wait_ge(mv2_made, T + 1)
                    power(var, var, eps2_added, rstd2_made, T, len(tiles))

                def list_tokens(bd, i):
                    group, par, _ = bd.finished(i, "route")
                    pool.wait_ge(placed, group + 1)
                    settle(pool)
                    for t in range(NT):
                        pool.indirect_dma_start(
                            out=list_d, out_offset=bass.IndirectOffsetOnAxis(
                                ap=place_i[:, par, t:t + 1].bitcast(U32), axis=0),
                            in_=tok_now[:, par, t:t + 1], in_offset=None, bounds_check=LIST - 1,
                            oob_is_err=False).then_inc(listed[par], 16)

                def do_jobs(bd, i, slot):
                    for job, arg in bd.jobs(i, slot):
                        if job == "stats":
                            patch(bd, arg)
                        elif job == "qk":
                            rope(bd, i, arg)
                        elif job == "trQ":
                            split(bd, i, arg)
                        elif job == "add":
                            statistics2(bd, i, arg)
                        elif job == "list":
                            list_tokens(bd, i)

                def prepare_lists():
                    for par in range(2):
                        pool.indirect_dma_start(
                            out=list_d, out_offset=bass.IndirectOffsetOnAxis(ap=nowhere[:, :].bitcast(U32), axis=0),
                            in_=nowhere[:, :], in_offset=None, bounds_check=LIST - 1,
                            oob_is_err=False).then_inc(listed[par], 16)
                    pool.wait_ge(rows_stored[0], 16)
                    pool.wait_ge(filled, 16 * (FILLS - 1))

                def run(bd):
                    for i in range(len(body_jobs(bd.kind))):
                        for slot in range(NH):
                            do_jobs(bd, i, slot)
                    if bd.kind == "prologue":
                        prepare_lists()

                pool.memset(half_neg[:, :], -0.5).then_inc(pool_set, 1)
                pool.memset(zero_row[:, :], 0.0).then_inc(pool_set, 1)
                pool.memset(nowhere[:, :], LIST).then_inc(pool_set, 1)
                pool.memset(sentinels[:, :], NTOK).then_inc(pool_set, 1)
                pool.wait_ge(pool_set, 4)
                pool.memset(kst[SK:SK + 2, :, :], 1.0).then_inc(consts_set, 1)
                pool.wait_ge(loaded, 16 * N_CONSTS)
                pool.wait_ge(consts_set, 5)
                pool.wait_ge(loaded, 16 * N_CONSTS)
                pool.wait_ge(consts_set, 5)
                all_bodies(pool, run)
                pool.wait_ge(listed[0], 16 * NT * (NG // 2) + 16)
                pool.wait_ge(listed[1], 16 * NT * (NG // 2) + 16)

        def s2(name, shape, dt=F32):
            return sb(name, shape, dt)

        count_i = s2("count_i", [1, 3, NE], I32)
        tiles_of = s2("tiles_of", [1, NE])
        tiles_f = s2("tiles_f", [1, 2, NE])
        past = s2("past", [1, 3, NFT])
        te = s2("te", [1, 3, NFT])
        idx = s2("idx", [128, NFT], I32)
        row_idx = s2("row_idx", [128, 2], I32)
        out_idx = s2("out_idx", [128, 2], I32)
        b2_sb = s2("b2_sb", [128, NE * E])
        got = s2("got", [128, 2, ROW])
        xn = s2("xn", [128, 2, E])
        hb = s2("hb", [128, 4, E])
        xnT = s2("xnT", [KC + 1, 2, 2, FT])
        act_h = s2("act_h", [128, 2, HID])
        hT = s2("hT", [128, PJ, FT])
        y = s2("y", [128, 2, E])
        h_bank = [whole.enter_context(nc.psum_tensor(f"h_bank{n}", [128, 2, 512], F32)) for n in range(2)]
        x_bank = whole.enter_context(nc.psum_tensor("x_bank", [128, 512], F32))
        t_bank = [whole.enter_context(nc.psum_tensor(f"t_bank{n}", [128, 512], F32)) for n in range(2)]
        y_bank = whole.enter_context(nc.psum_tensor("y_bank", [128, 512], F32))

        table_step = sem("table_step")
        table_made = sem("table_made")
        ones_set = sem("ones_set")
        b2_loaded = sem("b2_loaded")
        idx_in = [sem(f"idx_in{n}") for n in range(4)]
        row_idx_made = sem("row_idx_made")
        out_idx_made = sem("out_idx_made")
        gathered = [sem(f"gathered{p}") for p in range(2)]
        xn_made = sem("xn_made")
        hb_made = sem("hb_made")
        xT_written = sem("xT_written")
        xT_read = sem("xT_read")
        h_written = sem("h_written")
        gelu_made = sem("gelu_made")
        hT_written = sem("hT_written")
        hT_read = sem("hT_read")
        y_written = sem("y_written")
        y_made = sem("y_made")
        scattered = [sem(f"scattered{p}") for p in range(2)]

        def all_tiles(eng, run):
            for t in (0, 1):
                run(t, t, 0)
            with eng.Fori(0, (NFT - 6) // 4) as m:
                for j in range(2, 6):
                    run(m * 4 + j, j % 4, m + j // 4)
            for t in range(NFT - 4, NFT):
                run(t, t % 4, t // 4)

        def has_next(t, ahead=1):
            return not (isinstance(t, int) and t + ahead >= NFT)

        def has_former(t):
            return not (isinstance(t, int) and t == 0)

        def column(a, t):
            return a[:, t:t + 1] if isinstance(t, int) else a[:, bass.ds(t, 1)]

        def at(table, t):
            return table[0:1, t:t + 1] if isinstance(t, int) else table[0:1, bass.ds(t, 1)]

        block = whole.enter_context(nc.Block())

        @block.sync
        def _(sp):
            sp.dma_start(b2_sb[:], b2).then_inc(b2_loaded, 16)
            sp.wait_ge(table_made, 1)

            def run(t, slot, q):
                if not (isinstance(t, int) and t < 4):
                    sp.wait_ge(idx_in[slot], q * 16)
                place = sp.value_load(at(tile_place, t), min_val=0, max_val=LIST - FT)
                sp.dma_start(column(idx, t), list_d[bass.ds(place, FT), :]).then_inc(idx_in[slot], 16)

            for t in range(4):
                run(t, t, 0)
            with sp.Fori(1, NFT // 4) as m:
                for j in range(4):
                    run(m * 4 + j, j, m)
            for t in range(NFT - NFT % 4, NFT):
                run(t, t % 4, t // 4)

        @block.gpsimd
        def _(pool):
            def gather(t, slot, q):
                par, k = slot % 2, q * 2 + slot // 2
                pool.wait_ge(idx_in[slot], q * 16 + 16)
                if not (isinstance(t, int) and t < 2):
                    pool.wait_ge(gathered[par], k * 16)
                settle(pool)
                pool.tensor_copy(row_idx[:, par:par + 1], column(idx, t)).then_inc(row_idx_made, 1)
                pool.wait_ge(row_idx_made, t + 1)
                if not (isinstance(t, int) and t < 2):
                    pool.wait_ge(hb_made, t - 1)
                settle(pool)
                pool.indirect_dma_start(out=got[:, par, :], out_offset=None, in_=rows_d,
                                        in_offset=bass.IndirectOffsetOnAxis(
                                            ap=row_idx[:, par:par + 1].bitcast(U32), axis=0),
                                        bounds_check=NTOK, oob_is_err=False).then_inc(gathered[par], 16)

            def scatter(t, slot, k):
                par = slot % 2
                if not (isinstance(t, int) and t < 2):
                    pool.wait_ge(scattered[par], k * 16)
                settle(pool)
                pool.tensor_copy(out_idx[:, par:par + 1], column(idx, t)).then_inc(out_idx_made, 1)
                pool.wait_ge(out_idx_made, t + 1)
                pool.wait_ge(y_made, t + 1)
                settle(pool)
                pool.indirect_dma_start(out=out,
                                        out_offset=bass.IndirectOffsetOnAxis(
                                            ap=out_idx[:, par:par + 1].bitcast(U32), axis=0),
                                        in_=y[:, par, :], in_offset=None, bounds_check=NTOK - 1,
                                        oob_is_err=False).then_inc(scattered[par], 16)

            for t in range(3):
                gather(t, t, 0)

            def run(t, slot, q):
                if has_next(t, 3):
                    gather(t + 3, (slot + 3) % 4, q + (slot + 3) // 4)
                if has_former(t):
                    scatter(t - 1, (slot - 1) % 4, q * 2 + slot // 2 - 1 + slot % 2)

            all_tiles(pool, run)
            scatter(NFT - 1, (NFT - 1) % 4, (NFT - 1) // 2)
            pool.wait_ge(scattered[0], 16 * (NFT // 2))
            pool.wait_ge(scattered[1], 16 * (NFT // 2))

        @block.tensor
        def _(pe):
            pe.wait_ge(table_made, 1)
            pe.wait_ge(ones_set, 1)

            def expert(t):
                return pe.value_load(at(tile_expert, t), min_val=0, max_val=NE - 1)

            def tr_x(t, par):
                pe.wait_ge(xn_made, t + 1)
                wait(pe, xT_read, t)
                for c in range(2):
                    mm = pe.transpose(x_bank[0:KC, c * FT:(c + 1) * FT], xn[:, par, c * KC:(c + 1) * KC],
                                      ident[:, :])
                mm.then_inc(xT_written, 1)

            def up(t, par, e):
                pe.wait_ge(xT_read, t + 1)
                wait(pe, gelu_made, t - 1)
                for f in range(2):
                    for c in range(2):
                        rows = KC + c
                        mm = pe.matmul(h_bank[par][:, f, 0:HID // 2], xnT[0:rows, par, c, :],
                                       w1_sb[0:rows, bass.ds(e, 1), c, f * (HID // 2):(f + 1) * (HID // 2)]
                                       .rearrange("p e n -> p (e n)"), start=(c == 0), stop=(c == 1))
                mm.then_inc(h_written, 1)

            def tr_h(t, par):
                pe.wait_ge(gelu_made, t + 1)
                for b in range(2):
                    wait(pe, hT_read, 2 * t + b - 1)
                    for j in range(3):
                        a = (3 * b + j) * 128
                        mm = pe.transpose(t_bank[b][:, j * FT:(j + 1) * FT], act_h[:, par, a:a + 128], ident[:, :])
                    mm.then_inc(hT_written, 1)

            def down(t, e):
                wait(pe, y_made, t)
                for j in range(PJ):
                    if j % 3 == 0:
                        pe.wait_ge(hT_read, 2 * t + 1 + j // 3)
                    mm = pe.matmul(y_bank[:, 0:E], hT[:, j, :],
                                   w2_sb[:, bass.ds(e, 1), j, :].rearrange("p e n -> p (e n)"),
                                   start=(j == 0), stop=(j == PJ - 1))
                mm.then_inc(y_written, 1)

            tr_x(0, 0)

            def run(t, slot, q):
                par = slot % 2
                e = expert(t)
                if has_former(t):
                    former = expert(t - 1)
                    tr_h(t - 1, 1 - par)
                up(t, par, e)
                if has_next(t):
                    tr_x(t + 1, 1 - par)
                if has_former(t):
                    down(t - 1, former)

            all_tiles(pe, run)
            tr_h(NFT - 1, (NFT - 1) % 2)
            down(NFT - 1, expert(NFT - 1))

        @block.scalar
        def _(act):
            act.wait_ge(ones_set, 1)

            def read_x(t, par):
                act.wait_ge(xT_written, t + 1)
                wait(act, h_written, t - 1)
                act.activation(xnT[0:KC, par, :, :], x_bank[0:KC, 0:2 * FT].rearrange("p (c t) -> p c t", c=2),
                               ACT.Copy).then_inc(xT_read, 1)

            def run(t, slot, q):
                par = slot % 2
                act.wait_ge(h_written, t + 1)
                wait(act, hT_written, 2 * t - 2)
                act.activation(act_h[:, par, :].rearrange("p (f n) -> p f n", f=2),
                               h_bank[par][:, :, 0:HID // 2], ACT.Gelu).then_inc(gelu_made, 1)
                if has_next(t):
                    read_x(t + 1, 1 - par)

            read_x(0, 0)
            all_tiles(act, run)

        @block.vector
        def _(dve):
            n = [0]

            def step(ins):
                n[0] += 1
                ins.then_inc(table_step, 1)
                dve.wait_ge(table_step, n[0])

            step(dve.tensor_tensor(tiles_f[:, 0, :], places[0:1, :], base_sb[0:1, :], ALU.subtract))
            step(dve.tensor_scalar(count_i[:, 0, :], tiles_f[:, 0, :], float(FT - 1), None, ALU.add))
            step(dve.tensor_scalar(count_i[:, 1, :], count_i[:, 0, :], 7, None, ALU.arith_shift_right))
            step(dve.tensor_copy(tiles_of[:, :], count_i[:, 1, :]))
            step(dve.tensor_copy(tiles_f[:, 1, 0:1], tiles_of[:, 0:1]))
            for e in range(1, 3):
                step(dve.tensor_tensor(tiles_f[:, 1, e:e + 1], tiles_f[:, 1, e - 1:e], tiles_of[:, e:e + 1], ALU.add))
            for e in range(3):
                step(dve.tensor_scalar(past[:, e, :], tvec[:, :], tiles_f[:, 1, e:e + 1], None, ALU.is_ge))
            step(dve.tensor_tensor(te[:, 0, :], past[:, 0, :], past[:, 1, :], ALU.add))
            step(dve.tensor_tensor(te[:, 0, :], te[:, 0, :], past[:, 2, :], ALU.add))
            step(dve.tensor_copy(tile_expert[:, :], te[:, 0, :]))
            for e in range(3):
                step(dve.tensor_scalar(past[:, e, :], past[:, e, :], tiles_of[:, e:e + 1], None, ALU.mult))
            step(dve.tensor_tensor(te[:, 1, :], past[:, 0, :], past[:, 1, :], ALU.add))
            step(dve.tensor_tensor(te[:, 1, :], te[:, 1, :], past[:, 2, :], ALU.add))
            step(dve.tensor_tensor(te[:, 2, :], tvec[:, :], te[:, 1, :], ALU.subtract))
            step(dve.tensor_scalar(te[:, 2, :], te[:, 2, :], float(FT), None, ALU.mult))
            step(dve.tensor_scalar(te[:, 0, :], te[:, 0, :], float(CAP), None, ALU.mult))
            step(dve.tensor_tensor(te[:, 2, :], te[:, 2, :], te[:, 0, :], ALU.add))
            dve.tensor_copy(tile_place[:, :], te[:, 2, :]).then_inc(table_made, 1)
            dve.wait_ge(table_made, 1)
            dve.memset(xnT[KC:KC + 1, :, :, :], 1.0).then_inc(ones_set, 1)

            def read_row(t, slot, k, e):
                par = slot % 2
                dve.wait_ge(gathered[par], (k + 1) * 16)
                wait(dve, xT_written, t - 1)
                dve.tensor_scalar(xn[:, par, :], got[:, par, 0:E], got[:, par, E:E + 1], got[:, par, E + 1:E + 2],
                                  ALU.subtract, ALU.mult).then_inc(xn_made, 1)
                wait(dve, y_made, t - 3)
                dve.tensor_tensor(hb[:, slot, :], got[:, par, 0:E], b2_sb[:, bass.ds(e * E, E)],
                                  ALU.add).then_inc(hb_made, 1)

            def read_h(t):
                for b in range(2):
                    dve.wait_ge(hT_written, 2 * t + b + 1)
                    wait(dve, y_written, t)
                    dve.tensor_copy(hT[:, 3 * b:3 * b + 3, :],
                                    t_bank[b][:, 0:3 * FT].rearrange("p (j t) -> p j t", j=3)).then_inc(hT_read, 1)

            def finish(t, slot, k):
                dve.wait_ge(y_written, t + 1)
                dve.wait_ge(hb_made, t + 1)
                if not (isinstance(t, int) and t < 2):
                    dve.wait_ge(scattered[slot % 2], k * 16)
                dve.tensor_tensor(y[:, slot % 2, :], y_bank[:, 0:E], hb[:, slot, :], ALU.add).then_inc(y_made, 1)

            def expert(t):
                return dve.value_load(at(tile_expert, t), min_val=0, max_val=NE - 1)

            dve.wait_ge(b2_loaded, 16)
            for t in range(2):
                read_row(t, t, 0, expert(t))

            def run(t, slot, q):
                k = q * 2 + slot // 2
                if has_next(t, 2):
                    e = expert(t + 2)
                if has_former(t):
                    read_h(t - 1)
                if has_next(t, 2):
                    read_row(t + 2, (slot + 2) % 4, k + 1, e)
                if has_former(t):
                    finish(t - 1, (slot - 1) % 4, k - 1 + slot % 2)

            all_tiles(dve, run)
            read_h(NFT - 1)
            finish(NFT - 1, (NFT - 1) % 4, (NFT - 1) // 2)


N_CONSTS = 20


def kernel(x, L0_tok_W, L0_tok_b, L0_attn_wq, L0_attn_bq, L0_attn_wk, L0_attn_bk, L0_attn_wv, L0_attn_bv,
           L0_attn_wo, L0_attn_bo, L0_ffn_Wg, L0_ffn_bg, L0_ffn_W1, L0_ffn_b1, L0_ffn_W2, L0_ffn_b2):
    import concourse.bacc as bacc
    from concourse.bass_utils import run_bass_kernel_spmd

    def rows(a, n):
        return np.broadcast_to(np.asarray(a)[None], (n,) + np.shape(a))

    def chunks(w, k):
        w = np.asarray(w)
        return w.reshape(k, w.shape[0] // k, w.shape[1]).transpose(1, 0, 2)

    tokens = np.asarray(x).reshape(B, CH, SIDE, PATCH, SIDE, PATCH).transpose(0, 2, 4, 1, 3, 5).reshape(NTOK, PD)
    pos = np.arange(GT, dtype=np.float32) % TOK
    scale = np.float32(10000.0) ** (np.float32(2.0) * np.arange(4, dtype=np.float32) / np.float32(HD))
    angle = (pos[:, None] / scale[None]).astype(np.float32)
    cos, sin = np.cos(angle).astype(np.float32), np.sin(angle).astype(np.float32)
    tables = [np.stack([cos, cos], 1), np.stack([sin, -sin], 1)]
    tables = [a.reshape(NT, TP, 2, 4).transpose(1, 0, 2, 3) for a in tables]
    mask = np.ones((NE, NT), np.float32)
    mask[:, 0] = 0.0
    base = np.arange(NE, dtype=np.float32) * CAP - 1
    arrays = dict(
        xT=tokens.reshape(NTOK // TP, TP, PJ, 128).transpose(0, 3, 2, 1).reshape(NTOK // TP, 128, PJ * TP),
        wtok=chunks(np.asarray(L0_tok_W).T, PJ),
        wqk=chunks(np.concatenate([np.asarray(L0_attn_wq).T, np.asarray(L0_attn_wk).T], 1), 2),
        wv=chunks(np.asarray(L0_attn_wv).T, 2),
        wo=chunks(np.asarray(L0_attn_wo).T, 2),
        w1=np.asarray(L0_ffn_W1).reshape(NE, 2, KC, HID).transpose(2, 0, 1, 3),
        b1=np.asarray(L0_ffn_b1).reshape(1, NE, HID),
        w2=np.asarray(L0_ffn_W2).reshape(NE, PJ, 128, E).transpose(2, 0, 1, 3),
        btok=rows(L0_tok_b, TP),
        bqk=np.concatenate([np.asarray(L0_attn_bq), np.asarray(L0_attn_bk)])[None],
        bv=rows(L0_attn_bv, 1),
        bo=rows(L0_attn_bo, 1),
        wg=rows(np.asarray(L0_ffn_Wg).T, TP),
        bg=rows(L0_ffn_bg, TP),
        b2=rows(np.asarray(L0_ffn_b2).reshape(NE * E), 128),
        rope_cos=tables[0], rope_sin=tables[1],
        ident_in=np.eye(128, dtype=np.float32),
        tri_in=np.triu(np.ones((TP, TP), np.float32), 1),
        ones_in=np.ones((TP, TP), np.float32),
        scan_mask=rows(mask.reshape(-1), TP),
        desc_in=rows(np.arange(NE, 0, -1, dtype=np.float32), TP),
        base_in=rows(base, TP),
        tokid_in=(np.arange(GT, dtype=np.int32) - GT).reshape(NT, TP).T,
        tvec_in=np.arange(NFT, dtype=np.float32)[None],
    )
    nc = bacc.Bacc("TRN2", target_bir_lowering=False, num_devices=1)
    args, feeds = {}, {}
    for name, a in arrays.items():
        a = np.ascontiguousarray(a)
        feeds[name + "_dram"] = a
        args[name] = nc.dram_tensor(name + "_dram", a.shape, mybir.dt.from_np(a.dtype), kind="ExternalInput").ap()
    args["out"] = nc.dram_tensor("out_dram", (NTOK, E), F32, kind="ExternalOutput").ap()
    build(nc, **args)
    result = run_bass_kernel_spmd(nc, [feeds], core_ids=[0])
    return result.results[0]["out_dram"].reshape(B, TOK, E)
```
